# Optimizing a Trainium2 kernel written in Bass

```python
import numpy as np
import jax
import jax.numpy as jnp

def _softmax(x, axis=-1):
    return jax.nn.softmax(x, axis=axis)

def _gelu(x):
    return jax.nn.gelu(x, approximate=True)

def _silu(x):
    return jax.nn.silu(x)

def _sigmoid(x):
    return jax.nn.sigmoid(x)

def _layernorm(x, axis=-1, eps=1e-05):
    m = jnp.mean(x, axis=axis, keepdims=True)
    v = jnp.var(x, axis=axis, keepdims=True)
    return (x - m) / jnp.sqrt(v + eps)

def _scatter_add(tgt, idx, src, axis=0):
    return tgt.at[idx].add(src)

def _segment_sum(src, seg, n):
    return jax.ops.segment_sum(src, seg, n)
kernel_name = 'mk_audio_tower_d1_tok_audfeat256_r4_841843'

def setup_inputs(seed: int=0):
    np.random.seed(seed)
    _w = jnp.asarray

    def _rec_inputs():
        import jax
        import jax.numpy as jnp
        _rk = jax.random.key(seed)
        x = -0.00040386 + 0.999972 * jax.random.normal(jax.random.fold_in(_rk, 1), (64, 750, 64), jnp.float32)
        return x
    x = _rec_inputs()

    def _L0_tok_setup():
        import jax, jax.numpy as jnp
        import numpy as np
        LN_EPS = 1e-05
        key = jax.random.key(seed)
        ks = jax.random.split(key, 8)
        dim = 64
        b, n3 = (8, 1536)
        s = 0.02
        return {'x': jax.random.normal(ks[0], (b, n3, dim), jnp.float32), 'ln_g': jnp.ones((dim,), jnp.float32), 'ln_b': jnp.zeros((dim,), jnp.float32), 'Wq': jax.random.normal(ks[1], (dim, dim), jnp.float32) * s, 'bq': jax.random.normal(ks[2], (dim,), jnp.float32) * s, 'Wk': jax.random.normal(ks[3], (dim, dim), jnp.float32) * s, 'bk': jax.random.normal(ks[4], (dim,), jnp.float32) * s, 'Wv': jax.random.normal(ks[5], (dim, dim), jnp.float32) * s, 'bv': jax.random.normal(ks[6], (dim,), jnp.float32) * s, 'Wo': jax.random.normal(ks[7], (dim, dim), jnp.float32) * s, 'bo': jnp.zeros((dim,), jnp.float32), 'heads': 8}
    _L0_tok_all = _L0_tok_setup()
    _L0_tok_in = {k: v for k, v in _L0_tok_all.items() if k in ('ln_g', 'ln_b', 'Wq', 'bq', 'Wk', 'bk', 'Wv', 'bv', 'Wo', 'bo')}
    del _L0_tok_all

    def _L0_attn_setup():
        import jax, jax.numpy as jnp
        import numpy as np
        import math
        B, S, D = (4, 1024, 64)
        key = jax.random.key(seed)
        ks = jax.random.split(key, 9)
        s = 1.0 / math.sqrt(D)
        return {'src': jax.random.normal(ks[0], (B, S, D), dtype=jnp.float32), 'Wq': jax.random.normal(ks[1], (D, D), dtype=jnp.float32) * s, 'bq': jax.random.normal(ks[2], (D,), dtype=jnp.float32) * s, 'Wk': jax.random.normal(ks[3], (D, D), dtype=jnp.float32) * s, 'bk': jax.random.normal(ks[4], (D,), dtype=jnp.float32) * s, 'Wv': jax.random.normal(ks[5], (D, D), dtype=jnp.float32) * s, 'bv': jax.random.normal(ks[6], (D,), dtype=jnp.float32) * s, 'Wo': jax.random.normal(ks[7], (D, D), dtype=jnp.float32) * s, 'bo': jax.random.normal(ks[8], (D,), dtype=jnp.float32) * s}
    _L0_attn_all = _L0_attn_setup()
    _L0_attn_in = {k: v for k, v in _L0_attn_all.items() if k in ('Wq', 'bq', 'Wk', 'bk', 'Wv', 'bv', 'Wo', 'bo')}
    del _L0_attn_all

    def _L0_ffn_setup():
        import jax, jax.numpy as jnp
        import numpy as np
        B, K, D = (128, 16, 64)
        E = 32
        H = int(D * 0.25)
        key = jax.random.key(seed)
        ks = jax.random.split(key, 7)
        d_rs = D ** (-0.5)
        h_rs = H ** (-0.5)
        x = jax.random.normal(ks[0], (B, K, D), dtype=jnp.float32)
        router_w = jax.random.uniform(ks[1], (E, D), jnp.float32, -d_rs, d_rs)
        router_b = jax.random.uniform(ks[2], (E,), jnp.float32, -d_rs, d_rs)
        W1 = jax.random.uniform(ks[3], (E, D, H), jnp.float32, -h_rs, h_rs)
        b1 = jax.random.uniform(ks[4], (E, H), jnp.float32, -h_rs, h_rs)
        W2 = jax.random.uniform(ks[5], (E, H, D), jnp.float32, -d_rs, d_rs)
        b2 = jax.random.uniform(ks[6], (E, D), jnp.float32, -d_rs, d_rs)
        return {'x': x, 'router_w': router_w, 'router_b': router_b, 'W1': W1, 'b1': b1, 'W2': W2, 'b2': b2}
    _L0_ffn_all = _L0_ffn_setup()
    _L0_ffn_in = {k: v for k, v in _L0_ffn_all.items() if k in ('router_w', 'router_b', 'W1', 'b1', 'W2', 'b2')}
    del _L0_ffn_all
    return {'x': x, 'L0_tok_ln_g': _L0_tok_in['ln_g'], 'L0_tok_ln_b': _L0_tok_in['ln_b'], 'L0_tok_Wq': _L0_tok_in['Wq'], 'L0_tok_bq': _L0_tok_in['bq'], 'L0_tok_Wk': _L0_tok_in['Wk'], 'L0_tok_bk': _L0_tok_in['bk'], 'L0_tok_Wv': _L0_tok_in['Wv'], 'L0_tok_bv': _L0_tok_in['bv'], 'L0_tok_Wo': _L0_tok_in['Wo'], 'L0_tok_bo': _L0_tok_in['bo'], 'L0_attn_Wq': _L0_attn_in['Wq'], 'L0_attn_bq': _L0_attn_in['bq'], 'L0_attn_Wk': _L0_attn_in['Wk'], 'L0_attn_bk': _L0_attn_in['bk'], 'L0_attn_Wv': _L0_attn_in['Wv'], 'L0_attn_bv': _L0_attn_in['bv'], 'L0_attn_Wo': _L0_attn_in['Wo'], 'L0_attn_bo': _L0_attn_in['bo'], 'L0_ffn_router_w': _L0_ffn_in['router_w'], 'L0_ffn_router_b': _L0_ffn_in['router_b'], 'L0_ffn_W1': _L0_ffn_in['W1'], 'L0_ffn_b1': _L0_ffn_in['b1'], 'L0_ffn_W2': _L0_ffn_in['W2'], 'L0_ffn_b2': _L0_ffn_in['b2']}

def reference(x, L0_tok_ln_g, L0_tok_ln_b, L0_tok_Wq, L0_tok_bq, L0_tok_Wk, L0_tok_bk, L0_tok_Wv, L0_tok_bv, L0_tok_Wo, L0_tok_bo, L0_attn_Wq, L0_attn_bq, L0_attn_Wk, L0_attn_bk, L0_attn_Wv, L0_attn_bv, L0_attn_Wo, L0_attn_bo, L0_ffn_router_w, L0_ffn_router_b, L0_ffn_W1, L0_ffn_b1, L0_ffn_W2, L0_ffn_b2):
    import jax
    import jax.numpy as jnp

    def _L0_tok_ref(x, ln_g, ln_b, Wq, bq, Wk, bk, Wv, bv, Wo, bo, heads):
        import jax, jax.numpy as jnp
        import numpy as np
        LN_EPS = 1e-05
        dim = x.shape[-1]
        scale = dim ** (-0.5)
        d = dim // heads

        def cross_attn(xcat):
            mu = jnp.mean(xcat, axis=-1, keepdims=True)
            var = jnp.mean(jnp.square(xcat - mu), axis=-1, keepdims=True)
            xn = (xcat - mu) * jax.lax.rsqrt(var + LN_EPS) * ln_g + ln_b
            x1, x2 = jnp.split(xn, 2, axis=0)
            q = x1 @ Wq.T + bq
            k = x2 @ Wk.T + bk
            v = x2 @ Wv.T + bv
            b_, n_ = (q.shape[0], q.shape[1])
            q = q.reshape(b_, n_, heads, d).transpose(0, 2, 1, 3)
            k = k.reshape(b_, n_, heads, d).transpose(0, 2, 1, 3)
            v = v.reshape(b_, n_, heads, d).transpose(0, 2, 1, 3)
            dots = jnp.einsum('bhid,bhjd->bhij', q, k) * scale
            attn = jax.nn.softmax(dots, axis=-1)
            out = jnp.einsum('bhij,bhjd->bhid', attn, v)
            out = out.transpose(0, 2, 1, 3).reshape(b_, n_, dim)
            return out @ Wo.T + bo
        x_origin, x_emap, x_lbp = jnp.split(x, 3, axis=1)
        out_oe = cross_attn(jnp.concatenate((x_origin, x_emap), axis=0))
        out_ol = cross_attn(jnp.concatenate((x_origin, x_lbp), axis=0))
        return out_oe + out_ol

    def _L0_attn_ref(src, Wq, bq, Wk, bk, Wv, bv, Wo, bo):
        import jax, jax.numpy as jnp
        import numpy as np
        import math
        B, S, D = (4, 1024, 64)
        q = src @ Wq.T + bq
        k = src @ Wk.T + bk
        v = src @ Wv.T + bv
        row_mask = (q[:, :, 0] != 0) & (k[:, :, 0] != 0)
        mask = row_mask[:, :, None]
        scale = 1.0 / math.sqrt(D)
        scores = jnp.einsum('bid,bjd->bij', q, k) * scale
        scores = jnp.where(mask, scores, jnp.float32(-1000000000.0))
        prob = jax.nn.softmax(scores, axis=-1)
        prob = jnp.where(mask, prob, 0.0)
        out = jnp.einsum('bij,bjd->bid', prob, v)
        return out @ Wo.T + bo

    def _L0_ffn_ref(x, router_w, router_b, W1, b1, W2, b2):
        import jax, jax.numpy as jnp
        import numpy as np
        B, K, D = (128, 16, 64)
        E = 32
        H = int(D * 0.25)
        xf = x.reshape(-1, D)
        logits = xf @ router_w.T + router_b
        idx = jnp.argmax(logits, axis=-1)
        w1t = jnp.take(W1, idx, axis=0)
        h = jnp.einsum('nd,ndh->nh', xf, w1t) + jnp.take(b1, idx, axis=0)
        h = jax.nn.relu(h)
        w2t = jnp.take(W2, idx, axis=0)
        out = jnp.einsum('nh,nhd->nd', h, w2t) + jnp.take(b2, idx, axis=0)
        out = jax.nn.relu(out)
        return out.reshape(x.shape)
    h = _L0_tok_ref(x, L0_tok_ln_g, L0_tok_ln_b, L0_tok_Wq, L0_tok_bq, L0_tok_Wk, L0_tok_bk, L0_tok_Wv, L0_tok_bv, L0_tok_Wo, L0_tok_bo, 8)
    h = h + _L0_attn_ref(_layernorm(h, axis=-1), L0_attn_Wq, L0_attn_bq, L0_attn_Wk, L0_attn_bk, L0_attn_Wv, L0_attn_bv, L0_attn_Wo, L0_attn_bo)
    h = h + _L0_ffn_ref(_layernorm(h, axis=-1), L0_ffn_router_w, L0_ffn_router_b, L0_ffn_W1, L0_ffn_b1, L0_ffn_W2, L0_ffn_b2)
    return h

_drawn_inputs = setup_inputs


def setup_inputs(seed=0):
    import zlib

    import numpy as np

    out = dict(_drawn_inputs(seed))
    spreads = {'L0_tok_ln_g': (1.0, 0.6), 'L0_tok_ln_b': (0.0, 0.342), 'L0_tok_bo': (0.0, 0.1)}
    factors = {'x': 6.137,
     'L0_tok_Wq': 8.0,
     'L0_tok_bq': 8.0,
     'L0_tok_Wk': 8.0,
     'L0_tok_bk': 8.0,
     'L0_tok_Wv': 2.978,
     'L0_attn_Wq': 8.0,
     'L0_attn_bq': 8.0,
     'L0_attn_Wk': 8.0,
     'L0_attn_bk': 8.0,
     'L0_ffn_b1': 3.606}
    for name, (base, spread) in spreads.items():
        noise = np.random.default_rng([zlib.crc32(name.encode()), seed]).standard_normal(out[name].shape)
        drawn = base * np.exp(spread * noise) if base else spread * noise
        out[name] = jnp.asarray(drawn.astype(out[name].dtype))
    for name, factor in factors.items():
        out[name] = (out[name] * factor).astype(out[name].dtype)
    return out
```

```python
from contextlib import ExitStack

import concourse.bass as bass
from concourse import mybir
from concourse.alu_op_type import AluOpType as ALU

ACT = mybir.ActivationFunctionType
F32 = mybir.dt.float32
BF16 = mybir.dt.bfloat16
AX_X = mybir.AxisListType.X

BATCH = 64
P = 125
R = 2
NT = P * R
D = 64
HEADS = 8
DH = D // HEADS
SIDES = 2
UNITS = SIDES * HEADS
PAIRS = HEADS // 2
EXPERTS = 32
HID = 16
CHUNKS = EXPERTS * HID // 128
LN_EPS = 1e-5
SCALE = 0.125
SHIFT = 48
KROWS = SHIFT + 3 * SIDES
BUFS = 3
STAGES = "NABCDEF"
DEPTH = len(STAGES)

COLS = {}
_at = 0
for _name, _width in (("q1", D), ("k1", D), ("v1", D), ("o1", D), ("q2", D), ("k2", D), ("v2", D + 2),
                      ("o2", D), ("router", EXPERTS)):
    COLS[_name] = (_at, _at + _width)
    _at += _width
W65_COLS = _at


def audio_tower_kernel(nc, x, w65, ln_gb, w1aug, w2, b2aug, bo2, ident, expert_rank, shift_rows, out):
    with ExitStack() as ctx:
        def sb(name, shape, dt=F32):
            return ctx.enter_context(nc.sbuf_tensor(name, shape, dt))

        def bank(name):
            return ctx.enter_context(nc.psum_tensor(name, [128, 512], F32))

        def sem(name):
            return ctx.enter_context(nc.semaphore(name))

        def sems(name, n):
            return [sem(f"{name}{i}") for i in range(n)]

        q_parts = nc.dram_tensor("q_parts", (3, D, NT), BF16, kind="Internal").ap()
        k_parts = nc.dram_tensor("k_parts", (SIDES, 3, D, NT), BF16, kind="Internal").ap()
        shift_parts = nc.dram_tensor("shift_parts", (SIDES, 2, 3, PAIRS, NT), BF16, kind="Internal").ap()

        max_bank = [bank("max_bank0"), bank("max_bank1")]
        exp_bank = [bank("exp_bank0"), bank("exp_bank1")]
        o_bank = bank("o_bank")
        m0 = bank("m0")
        m1 = bank("m1")
        m2 = bank("m2")

        w_sb = sb("w_sb", [D + 1, W65_COLS])
        gb_sb = sb("gb_sb", [D, 2])
        w1_sb = sb("w1_sb", [128, EXPERTS * HID])
        w2_sb = sb("w2_sb", [128, CHUNKS, D])
        b2_sb = sb("b2_sb", [128, D])
        bo2_sb = sb("bo2_sb", [P, D])
        id32 = sb("id32", [128, 128])
        id16 = sb("id16", [128, 128], BF16)
        minus_half = sb("minus_half", [P, 1])
        rank_sb = sb("rank_sb", [P, EXPERTS])

        x_in = sb("x_in", [P, 3 * R, D])
        xc1 = sb("xc1", [P, 3 * R, D])
        sq1 = sb("sq1", [P, 3 * R, D])
        xn1 = sb("xn1", [P, 3 * R, D])
        st1 = sb("st1", [P, 5, 3 * R])
        x1T = sb("x1T", [D + 1, 3, NT])
        z_parts = sb("z_parts", [128, 6, NT], BF16)
        z_rest = sb("z_rest", [128, 2, NT])
        q_stack = [sb(f"q_stack{i}", [128, PAIRS, NT], BF16) for i in range(BUFS)]
        k_stack = [sb(f"k_stack{i}", [128, SIDES, PAIRS, NT], BF16) for i in range(BUFS)]
        v_aug = [sb(f"v_aug{i}", [P, SIDES * R, HEADS, 32]) for i in range(BUFS)]

        neg_max = sb("neg_max", [P, SIDES, R, HEADS])
        sh_parts = sb("sh_parts", [P, SIDES, R, 2, 3, PAIRS], BF16)
        sh_rest = sb("sh_rest", [P, SIDES, R, HEADS])
        sh_rows = sb("sh_rows", [2 * 3 * PAIRS, SIDES, NT], BF16)
        probs = sb("probs", [P, HEADS, R, NT])
        o_sb = sb("o_sb", [128, SIDES, 2, NT])

        recip1 = sb("recip1", [P, SIDES, 2, R, 4])
        on_side = sb("on_side", [P, SIDES, R, 2, 4, DH])
        on_sum = sb("on_sum", [P, R, D])
        onT = sb("onT", [D + 1, NT])
        h1 = sb("h1", [P, R, D])
        h1b = [sb(f"h1b{i}", [P, R, D]) for i in range(BUFS)]
        xc2 = sb("xc2", [P, R, D])
        sq2 = sb("sq2", [P, R, D])
        xn2 = sb("xn2", [P, R, D])
        st2 = sb("st2", [P, 5, R])

        x2T = sb("x2T", [D + 1, NT])
        qk2 = sb("qk2", [D, 2, NT])
        v2_sb = sb("v2_sb", [P, R, D])
        nonzero = sb("nonzero", [P, R, 2])
        row_mask = sb("row_mask", [P, R])
        neg_max2 = sb("neg_max2", [P, R])
        bias2 = sb("bias2", [P, R])
        sums2 = sb("sums2", [P, R])
        recip2 = sb("recip2", [P, R])
        row_scale = sb("row_scale", [P, R])
        p2 = sb("p2", [P, R, NT])
        p2T = sb("p2T", [P, R, NT])
        o2T = sb("o2T", [D, NT])
        h2 = [sb(f"h2_{i}", [P, R, D]) for i in range(BUFS)]
        xc3 = sb("xc3", [P, R, D])
        sq3 = sb("sq3", [P, R, D])
        xn3 = sb("xn3", [P, R, D])
        st3 = sb("st3", [P, 5, R])

        x3_rows = sb("x3_rows", [128, NT])
        one_hotT = sb("one_hotT", [128, NT])
        top = sb("top", [P, R])
        is_top = sb("is_top", [P, R, EXPERTS])
        top_rank = sb("top_rank", [P, R, EXPERTS])
        best_rank = sb("best_rank", [P, R])
        one_hot = sb("one_hot", [P, R, EXPERTS], BF16)
        hidden = sb("hidden", [128, CHUNKS, NT])
        y_sb = sb("y_sb", [P, R, D])

        consts_loaded = sem("consts_loaded")
        rows_set = sem("rows_set")
        zeros_set = sem("zeros_set")
        id16_ready = sem("id16_ready")
        x_loaded = sem("x_loaded")
        parts_stored = sem("parts_stored")
        stacks_loaded = sem("stacks_loaded")
        shift_stored = sems("shift_stored", SIDES)
        shift_loaded = sems("shift_loaded", SIDES)
        y_stored = sem("y_stored")

        def norm_sems(i):
            names = ("summed", "mean", "centered", "squared", "sumsq", "var", "rstd", "normed")
            return {n: sem(f"ln{i}_{n}") for n in names}

        ln1, ln2, ln3 = norm_sems(1), norm_sems(2), norm_sems(3)
        xT_kv_ready, xT_kv_taken = sem("xT_kv_ready"), sem("xT_kv_taken")
        xT_q_ready, xT_q_taken = sem("xT_q_ready"), sem("xT_q_taken")
        z_ready, z_high, z_rest_ready, z_mid, z_low = [sem(f"z_{n}") for n in ("ready", "high", "rest", "mid", "low")]
        v_ready, v_taken = sem("v_ready"), sem("v_taken")
        max_scores, max_done = sems("max_scores", HEADS), sems("max_done", HEADS)
        exp_scores, exp_done = sems("exp_scores", HEADS), sems("exp_done", HEADS)
        sh_high, sh_rest1, sh_mid, sh_low = [sems(f"sh_{n}", SIDES) for n in ("high", "rest", "mid", "low")]
        shT_ready, shT_taken = sems("shT_ready", SIDES), sems("shT_taken", SIDES)
        pv_done = sems("pv_done", 4)
        o_taken = sems("o_taken", SIDES)
        oT_ready = sems("oT_ready", SIDES)
        o_recip, o_normed = sems("o_recip", SIDES), sems("o_normed", SIDES)
        o_summed = sem("o_summed")
        onT_ready, onT_taken = sem("onT_ready"), sem("onT_taken")
        h1_ready, h1_taken, h1b_ready = sem("h1_ready"), sem("h1_taken"), sem("h1b_ready")
        x2T_ready, x2T_taken = sem("x2T_ready"), sem("x2T_taken")
        qk2_ready, qk2_taken = sem("qk2_ready"), sem("qk2_taken")
        v2_ready, v2_taken, nonzero_ready, mask_ready = [sem(n) for n in ("v2_ready", "v2_taken", "nonzero_ready", "mask_ready")]
        scores2_ready, max2_ready, bias2_ready, exp2_done = [sem(n) for n in ("scores2_ready", "max2_ready", "bias2_ready", "exp2_done")]
        p2T_ready, p2T_taken = sem("p2T_ready"), sem("p2T_taken")
        o2_ready, o2_taken = sem("o2_ready"), sem("o2_taken")
        recip2_ready, scale2_ready = sem("recip2_ready"), sem("scale2_ready")
        out2_ready, h2_ready = sem("out2_ready"), sem("h2_ready")
        x3T_ready, x3T_taken = sem("x3T_ready"), sem("x3T_taken")
        logits_ready, top_ready, logits_taken = sem("logits_ready"), sem("top_ready"), sem("logits_taken")
        rank_ready, best_ready, one_hot_ready = sem("rank_ready"), sem("best_ready"), sem("one_hot_ready")
        ohT_ready, ohT_taken = sem("ohT_ready"), sem("ohT_taken")
        hid_ready, relu_done = sems("hid_ready", 2), sems("relu_done", 2)
        out_ready, y_ready = sem("out_ready"), sem("y_ready")

        N_CONST_DMAS = 9 + BUFS * 2
        PARTS_DMAS, STACK_DMAS, SHIFT_LOADS = 3, 12, 2

        def wait(eng, semaphore, value):
            if isinstance(value, int) and value <= 0:
                return
            eng.wait_ge(semaphore, value)

        def unit_count(u, b):
            return b * SIDES + u // HEADS + 1

        def before(u, by):
            return (u - by) % UNITS, (u - by) // UNITS

        def batches(t, live):
            return [t - i for i in range(DEPTH)], lambda s: s in live

        def run(iteration, loop):
            fill = DEPTH - 1
            trips = (BATCH - fill) // BUFS
            for t in range(fill):
                iteration(t, t % BUFS, STAGES[:t + 1])
            with loop(fill, fill + trips * BUFS - (BUFS - 1), BUFS) as t:
                for k in range(BUFS):
                    iteration(t + k, k, STAGES)
            for t in range(fill + trips * BUFS, BATCH + fill):
                live = "".join(s for i, s in enumerate(STAGES) if 0 <= t - i < BATCH)
                iteration(t, t % BUFS, live)

        def weight(name):
            lo, hi = COLS[name]
            return w_sb[:, lo:hi]

        block = ctx.enter_context(nc.Block())

        @block.sync
        def _(sp):
            for dst, src in ((w_sb[:], w65), (gb_sb[:], ln_gb), (w1_sb[:], w1aug),
                             (w2_sb[:], w2.rearrange("(c p) d -> p c d", p=128)), (b2_sb[:], b2aug),
                             (bo2_sb[:], bo2.to_broadcast([P, D])), (id32[:], ident),
                             (rank_sb[:], expert_rank.to_broadcast([P, EXPERTS]))):
                sp.dma_start(dst, src).then_inc(consts_loaded, 16)
            for i in range(BUFS):
                for par in range(2):
                    sp.dma_start(k_stack[i][64 * par + SHIFT:64 * par + KROWS], shift_rows).then_inc(consts_loaded, 16)
            xs = x.rearrange("n (s p r) d -> n p s r d", s=3, r=R)
            ys = out.rearrange("n (p r) d -> n p r d", r=R)
            q_rows = q_parts.rearrange("a (i m g) c -> m (a i) g c", m=2, g=PAIRS)
            k_rows = k_parts.rearrange("s a (i m g) c -> m (a i) s g c", m=2, g=PAIRS)
            TERMS = ((0, 0, 24, 0), (24, 0, 16, 8), (40, 0, 8, 16))

            def shift_io(side, batch, k):
                wait(sp, shT_taken[side], batch + 1)
                sp.dma_start(shift_parts[side].rearrange("m a g c -> (m a g) c"),
                             sh_rows[:, side, :]).then_inc(shift_stored[side], 16)
                wait(sp, shift_stored[side], batch * 16 + 16)
                for par in range(2):
                    row = 64 * par + SHIFT + 3 * side
                    sp.dma_start(q_stack[k][row:row + 3], shift_parts[side, par]).then_inc(shift_loaded[side], 16)

            def iteration(t, k, live):
                (n, a, b, c, d, e, f), on = batches(t, live)
                if on("N"):
                    wait(sp, ln1["centered"], n)
                    sp.dma_start(x_in[:].rearrange("p (s r) d -> p s r d", r=R),
                                 xs[n] if isinstance(n, int) else xs[bass.ds(n, 1)].squeeze(0)).then_inc(x_loaded, 16)
                if on("C"):
                    shift_io(1, c, (k - 3) % BUFS)
                if on("A"):
                    ka = (k - 1) % BUFS
                    wait(sp, z_low, a + 1)
                    sp.dma_start(q_parts.rearrange("a r c -> r a c"), z_parts[0:D, 0:3, :]).then_inc(parts_stored, 16)
                    for side in range(SIDES):
                        sp.dma_start(k_parts[side].rearrange("a r c -> r a c"),
                                     z_parts[D * side:D * side + D, 3:6, :]).then_inc(parts_stored, 16)
                    wait(sp, parts_stored, a * (16 * PARTS_DMAS) + 16 * PARTS_DMAS)
                    for first, q0, rows, k0 in TERMS:
                        for par in range(2):
                            at = 64 * par + first
                            sp.dma_start(q_stack[ka][at:at + rows],
                                         q_rows[par, q0:q0 + rows]).then_inc(stacks_loaded, 16)
                            sp.dma_start(k_stack[ka][at:at + rows],
                                         k_rows[par, k0:k0 + rows]).then_inc(stacks_loaded, 16)
                if on("B"):
                    shift_io(0, b, (k - 2) % BUFS)
                if on("F"):
                    wait(sp, y_ready, f + 1)
                    sp.dma_start(ys[f] if isinstance(f, int) else ys[bass.ds(f, 1)].squeeze(0), y_sb[:]).then_inc(y_stored, 16)

            run(iteration, sp.Fori)
            sp.wait_ge(y_stored, 16 * BATCH)

        @block.tensor
        def _(pe):
            pe.wait_ge(consts_loaded, 16 * (N_CONST_DMAS - 1))
            pe.wait_ge(rows_set, 8)
            pe.wait_ge(zeros_set, 2 + BUFS)
            pe.wait_ge(id16_ready, 1)

            def max_unit(u, b, k):
                side, head = u // HEADS, u % HEADS
                at = 64 * (head % 2)
                if u == 0:
                    pe.wait_ge(stacks_loaded, b * (16 * STACK_DMAS) + 16 * STACK_DMAS)
                prior, back = before(u, 2)
                wait(pe, max_done[prior % HEADS], unit_count(prior, b + back))
                for r in range(R):
                    last = pe.matmul(max_bank[u % 2][0:P, r * NT:(r + 1) * NT],
                                     q_stack[k][at:at + SHIFT, head // 2, r * P:(r + 1) * P],
                                     k_stack[k][at:at + SHIFT, side, head // 2, :], start=True, stop=True)
                last.then_inc(max_scores[head], 1)

            def exp_unit(u, c, k):
                side, head = u // HEADS, u % HEADS
                at = 64 * (head % 2)
                rows = SHIFT + 3 * (side + 1)
                if u % HEADS == 0:
                    pe.wait_ge(shift_loaded[side], c * (16 * SHIFT_LOADS) + 16 * SHIFT_LOADS)
                prior, back = before(u, 2)
                wait(pe, exp_done[prior % HEADS], unit_count(prior, c + back))
                for kt in range(R):
                    last = pe.matmul(exp_bank[u % 2][0:P, kt * NT:(kt + 1) * NT],
                                     k_stack[k][at:at + rows, side, head // 2, kt * P:(kt + 1) * P],
                                     q_stack[k][at:at + rows, head // 2, :], start=True, stop=True)
                last.then_inc(exp_scores[head], 1)

            def pv(g, c, k):
                side, half = g // 2, g % 2
                wait(pe, exp_done[(4 * g + 3) % HEADS], unit_count(4 * g + 3, c))
                if g == 0:
                    wait(pe, v_taken, c + 1)
                    wait(pe, o_taken[1], c)
                if g == 2:
                    wait(pe, o_taken[0], c + 1)
                for kt in range(R):
                    for j in range(4):
                        head = 4 * half + j
                        last = pe.matmul(o_bank[32 * j:32 * j + 32, half * NT:(half + 1) * NT],
                                         v_aug[k][:, side * R + kt, head, :], probs[:, head, kt, :],
                                         start=(kt == 0), stop=(kt == R - 1), skip_group_check=True)
                last.then_inc(pv_done[g], 1)

            def transpose_tiles(dst, src, n):
                pe.matmul(dst[0:D, 0:P], src[:, 0, :], id32[0:P, 0:P], start=True, stop=True)
                for r in range(1, n):
                    last = pe.transpose(dst[0:D, r * P:(r + 1) * P], src[:, r, :], id32[0:P, 0:P])
                return last

            def iteration(t, k, live):
                (n, a, b, c, d, e, f), on = batches(t, live)
                kb, kc, kd = (k - 2) % BUFS, (k - 3) % BUFS, (k - 4) % BUFS
                wait(pe, y_ready, f)
                for slot in range(UNITS):
                    if on("C"):
                        exp_unit(slot, c, kc)
                    if on("B"):
                        max_unit(slot, b, kb)
                    if slot == 0 and on("A"):
                        wait(pe, ln1["normed"], a + 1)
                        wait(pe, v_taken, a)
                        transpose_tiles(m0, xn1[:, R:3 * R, :], 2 * R).then_inc(xT_kv_ready, 1)
                    if slot == 1:
                        if on("D"):
                            pv(3, d, kd)
                        if on("C"):
                            wait(pe, sh_low[1], c + 1)
                            wait(pe, shT_taken[0], c + 1)
                            if on("E"):
                                wait(pe, x2T_taken, e + 1)
                            shift_turn(1)
                        if on("A"):
                            wait(pe, xT_kv_taken, a + 1)
                            transpose_tiles(m0, xn1[:, 0:R, :], R).then_inc(xT_q_ready, 1)
                        if on("E"):
                            wait(pe, x2T_taken, e + 1)
                            wait(pe, h2_ready, e)
                            for i, w in enumerate(("q2", "k2")):
                                last = pe.matmul(m2[0:D, i * NT:(i + 1) * NT], weight(w), x2T[:], start=True, stop=True)
                            last.then_inc(qk2_ready, 1)
                    if slot == 2 and on("F"):
                        wait(pe, ln3["normed"], f + 1)
                        if on("A"):
                            wait(pe, xT_q_taken, a + 1)
                        transpose_tiles(m0, xn3, R).then_inc(x3T_ready, 1)
                    if slot == 3:
                        if on("A"):
                            wait(pe, xT_q_taken, a + 1)
                            if on("F"):
                                wait(pe, x3T_taken, f + 1)
                            for i, (w, section) in enumerate((("q1", 0), ("q1", 0), ("k1", 1), ("k1", 2))):
                                half = i % 2
                                last = pe.matmul(m0[D * half:D * half + D, (i // 2) * NT:(i // 2 + 1) * NT],
                                                 weight(w), x1T[:, section, :], start=True, stop=True,
                                                 skip_group_check=True)
                            last.then_inc(z_ready, 1)
                        if on("D"):
                            wait(pe, o_taken[0], d + 1)
                            if on("C"):
                                wait(pe, shT_taken[1], c + 1)
                            if on("E"):
                                wait(pe, x2T_taken, e + 1)
                            output_turn(0)
                        if on("E"):
                            wait(pe, qk2_taken, e + 1)
                            for r in range(R):
                                last = pe.matmul(m2[0:P, r * (D + 2):(r + 1) * (D + 2)], x2T[:, r * P:(r + 1) * P],
                                                 weight("v2"), start=True, stop=True)
                            last.then_inc(v2_ready, 1)
                    if slot == 5 and on("F"):
                        wait(pe, x3T_taken, f + 1)
                        if on("A"):
                            wait(pe, z_rest_ready, a + 1)
                        for r in range(R):
                            last = pe.matmul(m0[0:P, r * EXPERTS:(r + 1) * EXPERTS], x3_rows[0:D + 1, r * P:(r + 1) * P],
                                             weight("router"), start=True, stop=True)
                        last.then_inc(logits_ready, 1)
                    if slot == 5:
                        if on("C"):
                            pv(0, c, kc)
                        if on("D"):
                            wait(pe, o_taken[1], d + 1)
                            wait(pe, o_normed[0], d + 1)
                            output_turn(1)
                        if on("E"):
                            wait(pe, v2_taken, e + 1)
                            wait(pe, nonzero_ready, e + 1)
                            for r in range(R):
                                last = pe.matmul(m2[0:P, r * NT:(r + 1) * NT], qk2[:, 0, r * P:(r + 1) * P],
                                                 qk2[:, 1, :], start=True, stop=True)
                            last.then_inc(scores2_ready, 1)
                    if slot == 7 and on("A"):
                        wait(pe, z_rest_ready, a + 1)
                        if on("F"):
                            wait(pe, logits_taken, f + 1)
                        for j in range(SIDES * R):
                            last = pe.matmul(m0[0:P, j * D:(j + 1) * D], x1T[:, 1 + j // R, (j % R) * P:(j % R + 1) * P],
                                             weight("v1"), start=True, stop=True)
                        last.then_inc(v_ready, 1)
                    if slot == 7:
                        if on("D"):
                            wait(pe, o_summed, d + 1)
                            transpose_tiles(m1, on_sum, R).then_inc(onT_ready, 1)
                    if slot == 8 and on("F"):
                        wait(pe, one_hot_ready, f + 1)
                        if on("A"):
                            wait(pe, v_taken, a + 1)
                        for r in range(R):
                            last = pe.matmul(m0[96:128, r * P:(r + 1) * P], one_hot[:, r, :], id16[0:P, 0:P],
                                             start=True, stop=True)
                        last.then_inc(ohT_ready, 1)
                    if slot == 8 and on("E"):
                        wait(pe, exp2_done, e + 1)
                        for kt in range(R):
                            for r in range(R):
                                last = pe.transpose(m2[0:P, kt * NT + r * P:kt * NT + (r + 1) * P],
                                                    p2[:, r, kt * P:(kt + 1) * P], id32[0:P, 0:P])
                        last.then_inc(p2T_ready, 1)
                    if slot == 9:
                        if on("C"):
                            pv(1, c, kc)
                        if on("D"):
                            wait(pe, onT_taken, d + 1)
                            for r in range(R):
                                last = pe.matmul(m1[0:P, r * D:(r + 1) * D], onT[:, r * P:(r + 1) * P], weight("o1"),
                                                 start=True, stop=True)
                            last.then_inc(h1_ready, 1)
                    if slot == 10:
                        if on("F"):
                            wait(pe, ohT_taken, f + 1)
                            expert_in(0)
                        if on("B"):
                            wait(pe, sh_low[0], b + 1)
                            if on("C"):
                                wait(pe, shT_taken[1], c + 1)
                            if on("D"):
                                wait(pe, h1_taken, d + 1)
                            shift_turn(0)
                        if on("E"):
                            wait(pe, p2T_taken, e + 1)
                            for kt in range(R):
                                last = pe.matmul(m2[0:D, 0:NT], v2_sb[:, kt, :], p2T[:, kt, :],
                                                 start=(kt == 0), stop=(kt == R - 1))
                            last.then_inc(o2_ready, 1)
                    if slot == 11 and on("F"):
                        wait(pe, relu_done[0], f + 1)
                        expert_in(1)
                    if slot == 12 and on("E"):
                        wait(pe, o2_taken, e + 1)
                        for r in range(R):
                            last = pe.matmul(m2[0:P, r * D:(r + 1) * D], o2T[:, r * P:(r + 1) * P], weight("o2")[0:D],
                                             start=True, stop=True)
                        last.then_inc(out2_ready, 1)
                    if slot == 13:
                        if on("C"):
                            pv(2, c, kc)
                        if on("F"):
                            wait(pe, relu_done[1], f + 1)
                            for r in range(R):
                                for ch in range(CHUNKS):
                                    pe.matmul(m0[0:P, r * D:(r + 1) * D], hidden[:, ch, r * P:(r + 1) * P], w2_sb[:, ch, :],
                                              start=(ch == 0), stop=False)
                                last = pe.matmul(m0[0:P, r * D:(r + 1) * D], one_hotT[:, r * P:(r + 1) * P], b2_sb[:],
                                                 start=False, stop=True)
                            last.then_inc(out_ready, 1)
                    if slot == 15 and on("D"):
                        wait(pe, ln2["normed"], d + 1)
                        if on("B"):
                            wait(pe, shT_taken[0], b + 1)
                        transpose_tiles(m1, xn2, R).then_inc(x2T_ready, 1)

            def shift_turn(side):
                for r in range(R):
                    last = pe.matmul(m1[0:2 * 3 * PAIRS, r * P:(r + 1) * P],
                                     sh_parts[:, side, r].rearrange("p m a g -> p (m a g)"), id16[0:P, 0:P],
                                     start=True, stop=True)
                last.then_inc(shT_ready[side], 1)

            def output_turn(side):
                for half in range(2):
                    for r in range(R):
                        at = (half * R + r) * 128
                        last = pe.transpose(m1[0:P, at:at + 128], o_sb[:, side, half, r * P:(r + 1) * P], id32[:])
                last.then_inc(oT_ready[side], 1)

            def expert_in(i):
                for ch in range(2):
                    at = (2 * i + ch) * 128
                    last = pe.matmul(m0[:, ch * NT:(ch + 1) * NT], w1_sb[:, at:at + 128], x3_rows[:], start=True, stop=True)
                last.then_inc(hid_ready[i], 1)

            run(iteration, pe.Fori)

        @block.scalar
        def _(act):
            act.wait_ge(consts_loaded, 16 * (N_CONST_DMAS - 1))
            act.wait_ge(rows_set, 8)
            act.wait_ge(zeros_set, 2 + BUFS)

            def exp_unit(u, c):
                wait(act, exp_scores[u % HEADS], unit_count(u, c))
                if u % 4 == 0:
                    g = u // 4
                    wait(act, pv_done[(g + 2) % 4], c if g < 2 else c + 1)
                act.activation(probs[:, u % HEADS].rearrange("p k q -> p (k q)"), exp_bank[u % 2][0:P, 0:R * NT],
                               ACT.Exp, scale=SCALE).then_inc(exp_done[u % HEADS], 1)

            def shift_take(side, batch):
                wait(act, shT_ready[side], batch + 1)
                wait(act, shift_stored[side], batch * 16)
                act.copy(sh_rows[:, side, :], m1[0:2 * 3 * PAIRS, 0:NT]).then_inc(shT_taken[side], 1)

            def output_take(side, batch):
                wait(act, pv_done[2 * side + 1], batch + 1)
                wait(act, oT_ready[side], batch)
                act.copy(o_sb[:, side].rearrange("p h q -> p (h q)"), o_bank[:, 0:2 * NT]).then_inc(o_taken[side], 1)

            def iteration(t, k, live):
                (n, a, b, c, d, e, f), on = batches(t, live)
                for slot in range(UNITS):
                    if on("C"):
                        exp_unit(slot, c)
                    if slot == 0 and on("E"):
                        wait(act, x2T_ready, e + 1)
                        wait(act, v2_ready, e)
                        act.copy(x2T[0:D], m1[0:D, 0:NT]).then_inc(x2T_taken, 1)
                    if slot == 1 and on("A"):
                        wait(act, xT_kv_ready, a + 1)
                        wait(act, v_ready, a)
                        act.activation(x1T[0:D, 1:3].rearrange("p s c -> p (s c)"), m0[0:D, 0:2 * NT], ACT.Identity,
                                       bias=gb_sb[:, 1:2], scale=gb_sb[:, 0:1]).then_inc(xT_kv_taken, 1)
                    if slot == 2:
                        if on("A"):
                            wait(act, xT_q_ready, a + 1)
                            act.activation(x1T[0:D, 0], m0[0:D, 0:NT], ACT.Identity,
                                           bias=gb_sb[:, 1:2], scale=gb_sb[:, 0:1]).then_inc(xT_q_taken, 1)
                        if on("C"):
                            shift_take(1, c)
                        if on("D"):
                            output_take(1, d)
                        if on("E"):
                            wait(act, qk2_ready, e + 1)
                            wait(act, scores2_ready, e)
                            act.copy(qk2[:].rearrange("p i c -> p (i c)"), m2[0:D, 0:2 * NT]).then_inc(qk2_taken, 1)
                    if slot == 3 and on("F"):
                        wait(act, x3T_ready, f + 1)
                        wait(act, hid_ready[1], f)
                        act.copy(x3_rows[0:D], m0[0:D, 0:NT]).then_inc(x3T_taken, 1)
                    if slot == 4 and on("A"):
                        wait(act, z_ready, a + 1)
                        wait(act, parts_stored, a * (16 * PARTS_DMAS))
                        act.copy(z_parts[:, 0:6:5, :], m0[:, 0:2 * NT].rearrange("p (i c) -> p i c", i=2)).then_inc(z_high, 1)
                    if slot == 7:
                        if on("A"):
                            wait(act, v_ready, a + 1)
                            wait(act, pv_done[3], a - 2)
                            act.copy(v_aug[(k - 1) % BUFS][:, :, :, 0:DH],
                                     m0[0:P, 0:SIDES * R * D].rearrange("p (j h d) -> p j h d", h=HEADS, d=DH)
                                     ).then_inc(v_taken, 1)
                        if on("E"):
                            wait(act, bias2_ready, e + 1)
                            wait(act, p2T_ready, e)
                            wait(act, recip2_ready, e)
                            for r in range(R):
                                last = act.activation(p2[:, r, :], m2[0:P, r * NT:(r + 1) * NT], ACT.Exp,
                                                      bias=bias2[:, r:r + 1], scale=SCALE, accum_out=sums2[:, r:r + 1])
                            last.then_inc(exp2_done, 1)
                    if slot == 8:
                        if on("F"):
                            wait(act, ohT_ready, f + 1)
                            wait(act, out_ready, f)
                            act.copy(one_hotT[96:128], m0[96:128, 0:NT])
                            act.activation(x3_rows[96:128], m0[96:128, 0:NT], ACT.Copy, bias=-1.0).then_inc(ohT_taken, 1)
                        if on("D"):
                            wait(act, onT_ready, d + 1)
                            wait(act, h1_ready, d)
                            act.copy(onT[0:D], m1[0:D, 0:NT]).then_inc(onT_taken, 1)
                    if slot == 10:
                        if on("C"):
                            output_take(0, c)
                        if on("F"):
                            expert_relu(0, f)
                    if slot == 11:
                        if on("B"):
                            shift_take(0, b)
                        if on("E"):
                            wait(act, o2_ready, e + 1)
                            wait(act, out2_ready, e)
                            act.copy(o2T[:], m2[0:D, 0:NT]).then_inc(o2_taken, 1)
                    if slot == 12 and on("F"):
                        expert_relu(1, f)

            def expert_relu(i, f):
                wait(act, hid_ready[i], f + 1)
                wait(act, out_ready, f)
                act.activation(hidden[:, 2 * i:2 * i + 2].rearrange("p h c -> p (h c)"), m0[:, 0:2 * NT],
                               ACT.Relu).then_inc(relu_done[i], 1)

            run(iteration, act.Fori)

        @block.vector
        def _(dve):
            dve.memset(x1T[D:D + 1], 1.0).then_inc(rows_set, 1)
            dve.memset(onT[D:D + 1], 2.0).then_inc(rows_set, 1)
            dve.memset(minus_half[:], -0.5).then_inc(zeros_set, 1)
            dve.memset(x2T[D:D + 1], 1.0).then_inc(rows_set, 1)
            dve.memset(x3_rows[64:96], 1.0).then_inc(rows_set, 1)
            dve.memset(one_hotT[0:96], 0.0).then_inc(zeros_set, 1)
            for i in range(BUFS):
                dve.memset(v_aug[i][:], 0.0).then_inc(zeros_set, 1)
            dve.wait_ge(zeros_set, 2 + BUFS)
            for i in range(BUFS):
                dve.memset(v_aug[i][:, :, :, DH:DH + 1], 1.0).then_inc(rows_set, 1)
            dve.wait_ge(consts_loaded, 16 * (N_CONST_DMAS - 1))
            dve.tensor_copy(id16[:], id32[:]).then_inc(id16_ready, 1)
            dve.memset(h1[:], 0.0).then_inc(rows_set, 1)

            def norm_sum(ln, src, st, b):
                wait(dve, ln["centered"], b)
                dve.reduce_sum(st[:, 0], src, axis=AX_X).then_inc(ln["summed"], 1)
                dve.wait_ge(ln["summed"], b + 1)
                dve.tensor_scalar(st[:, 1], st[:, 0], -1.0 / D, None, ALU.mult).then_inc(ln["mean"], 1)

            def norm_var(ln, sq, st, b):
                dve.wait_ge(ln["squared"], b + 1)
                wait(dve, ln["normed"], b)
                dve.reduce_sum(st[:, 2], sq[:], axis=AX_X).then_inc(ln["sumsq"], 1)
                dve.wait_ge(ln["sumsq"], b + 1)
                dve.tensor_scalar(st[:, 3], st[:, 2], 1.0 / D, LN_EPS, ALU.mult, ALU.add).then_inc(ln["var"], 1)

            def max_unit(u, b):
                side, head = u // HEADS, u % HEADS
                at = (head % 2) * PAIRS + head // 2
                dve.wait_ge(max_scores[head], unit_count(u, b))
                dve.tensor_reduce(neg_max[:, side, :, at], max_bank[u % 2][0:P, 0:R * NT].rearrange("p (r c) -> p r c", r=R),
                                  AX_X, ALU.max, negate=True).then_inc(max_done[head], 1)

            def shift_split(side, b):
                nm = neg_max[:, side].rearrange("p r (m g) -> p r m g", g=PAIRS)
                rest = sh_rest[:, side].rearrange("p r (m g) -> p r m g", g=PAIRS)
                high, mid, low = [sh_parts[:, side, :, :, i, :] for i in range(3)]
                dve.wait_ge(max_done[HEADS - 1], unit_count(side * HEADS + HEADS - 1, b))
                wait(dve, shT_ready[side], b)
                dve.tensor_copy(high, nm).then_inc(sh_high[side], 1)
                dve.wait_ge(sh_high[side], b + 1)
                dve.tensor_tensor(rest, nm, high, ALU.subtract).then_inc(sh_rest1[side], 1)
                dve.wait_ge(sh_rest1[side], b + 1)
                dve.tensor_copy(mid, rest).then_inc(sh_mid[side], 1)
                dve.wait_ge(sh_mid[side], b + 1)
                dve.tensor_tensor(low, rest, mid, ALU.subtract).then_inc(sh_low[side], 1)

            def output_norm(side, d):
                o = m1[0:P, :].rearrange("p (h r j q) -> p h r j q", h=2, r=R, q=32)
                dve.wait_ge(oT_ready[side], d + 1)
                dve.reciprocal(recip1[:, side].rearrange("p h r j -> p (h r j)"),
                               m1[0:P, :].rearrange("p (n q) -> p n q", q=32)[:, :, DH]).then_inc(o_recip[side], 1)
                dve.wait_ge(o_recip[side], d + 1)
                for half in range(2):
                    last = dve.tensor_tensor(on_side[:, side, :, half], o[:, half, :, :, 0:DH],
                                             recip1[:, side, half].unsqueeze(3).to_broadcast([P, R, 4, DH]), ALU.mult)
                last.then_inc(o_normed[side], 1)

            def iteration(t, k, live):
                (n, a, b, c, d, e, f), on = batches(t, live)
                for slot in range(UNITS):
                    if slot == 0 and on("C"):
                        shift_split(1, c)
                    if on("B"):
                        max_unit(slot, b)
                    if slot == 0 and on("N"):
                        dve.wait_ge(x_loaded, n * 16 + 16)
                        norm_sum(ln1, x_in[:], st1, n)
                    if slot == 4:
                        if on("N"):
                            norm_var(ln1, sq1, st1, n)
                        if on("D"):
                            output_norm(0, d)
                        if on("E"):
                            v2 = m2[0:P, 0:R * (D + 2)].rearrange("p (r c) -> p r c", r=R)
                            dve.wait_ge(v2_ready, e + 1)
                            wait(dve, o2_ready, e)
                            dve.tensor_copy(v2_sb[:], v2[:, :, 0:D]).then_inc(v2_taken, 1)
                            dve.tensor_scalar(nonzero[:], v2[:, :, D:D + 2], 0.0, None, ALU.not_equal).then_inc(nonzero_ready, 1)
                            dve.wait_ge(nonzero_ready, e + 1)
                            dve.tensor_tensor(row_mask[:], nonzero[:, :, 0], nonzero[:, :, 1], ALU.mult).then_inc(mask_ready, 1)
                    if slot == 5:
                        if on("A"):
                            z = m0[:, 0:2 * NT].rearrange("p (i c) -> p i c", i=2)
                            dve.wait_ge(z_high, a + 1)
                            wait(dve, z_low, a)
                            dve.tensor_tensor(z_rest[:], z, z_parts[:, 0:6:5, :], ALU.subtract).then_inc(z_rest_ready, 1)
                            dve.wait_ge(z_rest_ready, a + 1)
                            dve.tensor_copy(z_parts[:, 1:5:3, :], z_rest[:]).then_inc(z_mid, 1)
                    if slot == 6:
                        if on("F"):
                            route(f)
                        if on("D"):
                            output_norm(1, d)
                            dve.wait_ge(o_normed[1], d + 1)
                            wait(dve, onT_ready, d)
                            s0, s1 = [on_side[:, s].rearrange("p r h j q -> p (r h j q)") for s in range(SIDES)]
                            dve.tensor_tensor(on_sum[:].rearrange("p r c -> p (r c)"), s0, s1, ALU.add).then_inc(o_summed, 1)
                        if on("E"):
                            dve.wait_ge(scores2_ready, e + 1)
                            dve.tensor_reduce(neg_max2[:], m2[0:P, 0:R * NT].rearrange("p (r c) -> p r c", r=R), AX_X,
                                              ALU.max, negate=True).then_inc(max2_ready, 1)
                            dve.wait_ge(max2_ready, e + 1)
                            wait(dve, exp2_done, e)
                            dve.tensor_scalar(bias2[:], neg_max2[:], SCALE, None, ALU.mult).then_inc(bias2_ready, 1)
                    if slot == 8 and on("B"):
                        shift_split(0, b)
                    if slot == 9 and on("E"):
                        dve.wait_ge(p2T_ready, e + 1)
                        wait(dve, o2_ready, e)
                        dve.tensor_copy(p2T[:].rearrange("p k q -> p (k q)"), m2[0:P, 0:R * NT]).then_inc(p2T_taken, 1)
                        dve.wait_ge(exp2_done, e + 1)
                        dve.reciprocal(recip2[:], sums2[:]).then_inc(recip2_ready, 1)
                        dve.wait_ge(recip2_ready, e + 1)
                        dve.wait_ge(mask_ready, e + 1)
                        dve.tensor_tensor(row_scale[:], recip2[:], row_mask[:], ALU.mult).then_inc(scale2_ready, 1)
                    if slot == 10 and on("D"):
                        dve.wait_ge(h1_ready, d + 1)
                        wait(dve, ln2["centered"], d)
                        wait(dve, h1b_ready, d)
                        dve.tensor_copy(h1[:].rearrange("p r c -> p (r c)"), m1[0:P, 0:R * D]).then_inc(h1_taken, 1)
                        dve.wait_ge(h1_taken, d + 1)
                        norm_sum(ln2, h1[:], st2, d)
                    if slot == 12 and on("D"):
                        norm_var(ln2, sq2, st2, d)
                    if slot == 13 and on("E"):
                        ke = (k - 5) % BUFS
                        dve.wait_ge(out2_ready, e + 1)
                        dve.wait_ge(scale2_ready, e + 1)
                        dve.wait_ge(h1b_ready, e + 1)
                        for r in range(R):
                            last = dve.scalar_tensor_tensor(out=h2[ke][:, r, :], in0=m2[0:P, r * D:(r + 1) * D],
                                                            scalar=row_scale[:, r:r + 1], in1=h1b[ke][:, r, :],
                                                            op0=ALU.mult, op1=ALU.add)
                        last.then_inc(h2_ready, 1)
                        dve.wait_ge(h2_ready, e + 1)
                        norm_sum(ln3, h2[ke][:], st3, e)
                    if slot == 14 and on("F"):
                        dve.wait_ge(out_ready, f + 1)
                        wait(dve, y_stored, f * 16)
                        dve.scalar_tensor_tensor(out=y_sb[:].rearrange("p r c -> p (r c)"), in0=m0[0:P, 0:R * D], scalar=0.0,
                                                 in1=h2[(k - 6) % BUFS][:].rearrange("p r c -> p (r c)"),
                                                 op0=ALU.max, op1=ALU.add).then_inc(y_ready, 1)
                    if slot == 15 and on("E"):
                        norm_var(ln3, sq3, st3, e)

            def route(f):
                logits = m0[0:P, 0:R * EXPERTS].rearrange("p (r e) -> p r e", r=R)
                dve.wait_ge(logits_ready, f + 1)
                dve.reduce_max(top[:], logits, axis=AX_X).then_inc(top_ready, 1)
                dve.wait_ge(top_ready, f + 1)
                dve.tensor_tensor(is_top[:], logits, top[:].unsqueeze(2).to_broadcast([P, R, EXPERTS]),
                                  ALU.is_equal).then_inc(logits_taken, 1)
                dve.wait_ge(logits_taken, f + 1)
                dve.tensor_tensor(top_rank[:], is_top[:], rank_sb[:].unsqueeze(1).to_broadcast([P, R, EXPERTS]),
                                  ALU.mult).then_inc(rank_ready, 1)
                dve.wait_ge(rank_ready, f + 1)
                dve.reduce_max(best_rank[:], top_rank[:], axis=AX_X).then_inc(best_ready, 1)
                dve.wait_ge(best_ready, f + 1)
                wait(dve, ohT_ready, f)
                dve.tensor_tensor(one_hot[:], top_rank[:], best_rank[:].unsqueeze(2).to_broadcast([P, R, EXPERTS]),
                                  ALU.is_equal).then_inc(one_hot_ready, 1)

            run(iteration, dve.Fori)

        @block.gpsimd
        def _(pool):
            pool.wait_ge(consts_loaded, 16 * (N_CONST_DMAS - 1))
            pool.wait_ge(zeros_set, 2 + BUFS)

            def norm_center(ln, src, xc, sq, st, groups, b):
                pool.wait_ge(ln["mean"], b + 1)
                wait(pool, ln["normed"], b)
                pool.tensor_tensor(xc[:], src, st[:, 1].unsqueeze(2).to_broadcast([P, groups, D]),
                                   ALU.add).then_inc(ln["centered"], 1)
                pool.wait_ge(ln["centered"], b + 1)
                wait(pool, ln["sumsq"], b)
                pool.tensor_tensor(sq[:], xc[:], xc[:], ALU.mult).then_inc(ln["squared"], 1)

            def norm_scale(ln, xc, xn, st, groups, b, read):
                pool.wait_ge(ln["var"], b + 1)
                pool.tensor_tensor(st[:, 4], st[:, 3], minus_half[:].to_broadcast([P, groups]),
                                   ALU.pow).then_inc(ln["rstd"], 1)
                pool.wait_ge(ln["rstd"], b + 1)
                wait(pool, read, b)
                pool.tensor_tensor(xn[:], xc[:], st[:, 4].unsqueeze(2).to_broadcast([P, groups, D]),
                                   ALU.mult).then_inc(ln["normed"], 1)

            def iteration(t, k, live):
                (n, a, b, c, d, e, f), on = batches(t, live)
                if on("N"):
                    norm_center(ln1, x_in[:], xc1, sq1, st1, 3 * R, n)
                if on("A"):
                    pool.wait_ge(z_mid, a + 1)
                    pool.tensor_tensor(z_parts[:, 2:4, :], z_rest[:], z_parts[:, 1:5:3, :], ALU.subtract).then_inc(z_low, 1)
                if on("N"):
                    norm_scale(ln1, xc1, xn1, st1, 3 * R, n, xT_q_ready)
                if on("D"):
                    pool.wait_ge(h1_taken, d + 1)
                    wait(pool, h2_ready, d - 2)
                    pool.tensor_tensor(h1b[(k - 4) % BUFS][:], h1[:], bo2_sb[:].unsqueeze(1).to_broadcast([P, R, D]),
                                       ALU.add).then_inc(h1b_ready, 1)
                    norm_center(ln2, h1[:], xc2, sq2, st2, R, d)
                    norm_scale(ln2, xc2, xn2, st2, R, d, x2T_ready)
                if on("E"):
                    norm_center(ln3, h2[(k - 5) % BUFS][:], xc3, sq3, st3, R, e)
                    norm_scale(ln3, xc3, xn3, st3, R, e, x3T_ready)

            run(iteration, pool.Fori)


def kernel(**inputs):
    import numpy as np
    import concourse.bacc as bacc
    from concourse.bass_utils import run_bass_kernel_spmd

    a = {name: np.asarray(value) for name, value in inputs.items()}

    def with_bias(w, b):
        return np.concatenate([w.T, b[None, :]], axis=0)

    def by_stack_row(w):
        return w.reshape(D + 1, PAIRS, 2, DH).transpose(0, 3, 2, 1).reshape(D + 1, D)

    q2 = with_bias(a["L0_attn_Wq"], a["L0_attn_bq"])
    k2 = with_bias(a["L0_attn_Wk"], a["L0_attn_bk"])
    w65 = np.concatenate([
        by_stack_row(with_bias(a["L0_tok_Wq"], a["L0_tok_bq"])),
        by_stack_row(with_bias(a["L0_tok_Wk"], a["L0_tok_bk"])),
        with_bias(a["L0_tok_Wv"], a["L0_tok_bv"]),
        with_bias(a["L0_tok_Wo"], a["L0_tok_bo"]),
        q2, k2,
        with_bias(a["L0_attn_Wv"], a["L0_attn_bv"]), q2[:, 0:1], k2[:, 0:1],
        with_bias(a["L0_attn_Wo"], a["L0_attn_bo"]),
        with_bias(a["L0_ffn_router_w"], a["L0_ffn_router_b"]),
    ], axis=1)
    expand = np.kron(np.eye(EXPERTS, dtype=np.float32), np.full((1, HID), 2.0 ** 126, np.float32))
    w1 = a["L0_ffn_W1"].transpose(1, 0, 2).reshape(D, EXPERTS * HID)
    w1aug = np.concatenate([w1, a["L0_ffn_b1"].reshape(1, -1), np.zeros((31, EXPERTS * HID), np.float32), expand])
    b2aug = np.concatenate([np.zeros((96, D), np.float32), a["L0_ffn_b2"]])
    shift_rows = np.zeros((3 * SIDES, SIDES, PAIRS, NT), np.float32)
    for side in range(SIDES):
        shift_rows[3 * side:3 * side + 3, side] = 1.0
    arrays = {
        "x": a["x"], "w65": w65, "ln_gb": np.stack([a["L0_tok_ln_g"], a["L0_tok_ln_b"]], axis=1),
        "w1aug": w1aug, "w2": a["L0_ffn_W2"].reshape(EXPERTS * HID, D), "b2aug": b2aug,
        "bo2": a["L0_attn_bo"][None, :], "ident": np.eye(128, dtype=np.float32),
        "expert_rank": np.arange(EXPERTS, 0, -1, dtype=np.float32)[None, :],
        "shift_rows": shift_rows.astype(mybir.dt.np(BF16)),
    }
    arrays = {name: np.ascontiguousarray(v) for name, v in arrays.items()}
    nc = bacc.Bacc("TRN2", target_bir_lowering=False, num_devices=1)
    args = [nc.dram_tensor(name, v.shape, mybir.dt.from_np(v.dtype), kind="ExternalInput").ap()
            for name, v in arrays.items()]
    out = nc.dram_tensor("out", (BATCH, NT, D), F32, kind="ExternalOutput").ap()
    audio_tower_kernel(nc, *args, out)
    result = run_bass_kernel_spmd(nc, [arrays], core_ids=[0])
    return result.results[0]["out"]
```

```python
from contextlib import ExitStack

import concourse.bass as bass
from concourse import mybir
from concourse.alu_op_type import AluOpType as ALU

ACT = mybir.ActivationFunctionType
F32 = mybir.dt.float32
BF16 = mybir.dt.bfloat16
AX_X = mybir.AxisListType.X

BATCH = 64
P = 125
R = 2
NT = P * R
D = 64
HEADS = 8
DH = D // HEADS
SIDES = 2
UNITS = SIDES * HEADS
PAIRS = HEADS // 2
EXPERTS = 32
HID = 16
CHUNKS = EXPERTS * HID // 128
LN_EPS = 1e-5
SCALE = 0.125
SHIFT = 48
KROWS = SHIFT + 3 * SIDES
BUFS = 3
STAGES = "NABCDEF"
DEPTH = len(STAGES)

COLS = {}
_at = 0
for _name, _width in (("q1", D), ("k1", D), ("v1", D), ("o1", D), ("v2", D + 2),
                      ("router", EXPERTS)):
    COLS[_name] = (_at, _at + _width)
    _at += _width
W65_COLS = _at


def audio_tower_kernel(nc, x, w65, ln_gb, w1aug, w2, b2, qk2_w, o2_w, bo2, ident, expert_rank, shift_rows, out):
    with ExitStack() as ctx:
        def sb(name, shape, dt=F32):
            return ctx.enter_context(nc.sbuf_tensor(name, shape, dt))

        def bank(name):
            return ctx.enter_context(nc.psum_tensor(name, [128, 512], F32))

        def sem(name):
            return ctx.enter_context(nc.semaphore(name))

        def sems(name, n):
            return [sem(f"{name}{i}") for i in range(n)]

        q_parts = nc.dram_tensor("q_parts", (3, D, NT), BF16, kind="Internal").ap()
        k_parts = nc.dram_tensor("k_parts", (SIDES, 3, D, NT), BF16, kind="Internal").ap()
        shift_parts = nc.dram_tensor("shift_parts", (SIDES, 2, 3, PAIRS, NT), BF16, kind="Internal").ap()

        max_bank = [bank("max_bank0"), bank("max_bank1")]
        exp_bank = [bank("exp_bank0"), bank("exp_bank1")]
        o_bank = bank("o_bank")
        m0 = bank("m0")
        m1 = bank("m1")
        m2 = bank("m2")

        w_sb = sb("w_sb", [D + 1, W65_COLS])
        gb_sb = sb("gb_sb", [D, 2])
        w1_sb = sb("w1_sb", [128, EXPERTS * HID])
        w2_sb = sb("w2_sb", [128, CHUNKS, D])
        b2_rep = sb("b2_rep", [3 * EXPERTS, D])
        b2_rest = sb("b2_rest", [3 * EXPERTS, D])
        b2_mid = sb("b2_mid", [3 * EXPERTS, D], BF16)
        b2_parts = sb("b2_parts", [3 * EXPERTS, D], BF16)
        qk2_w_sb = sb("qk2_w_sb", [D, 2, D + 1])
        a2_sb = sb("a2_sb", [D + 1, D + 1])
        o2_w_sb = sb("o2_w_sb", [2 * D, D])
        bo2_sb = sb("bo2_sb", [P, D])
        id32 = sb("id32", [128, 128])
        id16 = sb("id16", [128, 128], BF16)
        minus_half = sb("minus_half", [P, 1])
        rank_sb = sb("rank_sb", [P, EXPERTS])

        x_in = sb("x_in", [P, 3 * R, D])
        xc1 = sb("xc1", [P, 3 * R, D])
        sq1 = sb("sq1", [P, 3 * R, D])
        xn1 = sb("xn1", [P, 3 * R, D])
        st1 = sb("st1", [P, 5, 3 * R])
        x1T = sb("x1T", [D + 1, 3, NT])
        z_parts = sb("z_parts", [128, 6, NT], BF16)
        z_rest = sb("z_rest", [128, 2, NT])
        q_stack = [sb(f"q_stack{i}", [128, PAIRS, NT], BF16) for i in range(BUFS)]
        k_stack = [sb(f"k_stack{i}", [128, SIDES, PAIRS, NT], BF16) for i in range(BUFS)]
        v_aug = [sb(f"v_aug{i}", [P, SIDES * R, HEADS, 32]) for i in range(BUFS)]

        neg_max = sb("neg_max", [P, SIDES, R, HEADS])
        sh_parts = sb("sh_parts", [P, SIDES, R, 2, 3, PAIRS], BF16)
        sh_rest = sb("sh_rest", [P, SIDES, R, HEADS])
        sh_rows = sb("sh_rows", [2 * 3 * PAIRS, SIDES, NT], BF16)
        probs = sb("probs", [P, HEADS, R, NT])
        o_sb = sb("o_sb", [128, SIDES, 2, NT])

        recip1 = sb("recip1", [P, SIDES, 2, R, 4])
        on_side = sb("on_side", [P, SIDES, R, 2, 4, DH])
        on_sum = sb("on_sum", [P, R, D])
        onT = sb("onT", [D + 1, NT])
        h1 = sb("h1", [P, R, D])
        h1b = [sb(f"h1b{i}", [P, R, D]) for i in range(BUFS)]
        xc2 = sb("xc2", [P, R, D])
        sq2 = sb("sq2", [P, R, D])
        xn2 = sb("xn2", [P, R, D])
        st2 = sb("st2", [P, 5, R])

        x2T = sb("x2T", [D + 1, NT])
        qk2 = sb("qk2", [D + 1, NT])
        v2_sb = sb("v2_sb", [P, R, D])
        nonzero = sb("nonzero", [P, R, 2])
        row_mask = sb("row_mask", [P, R])
        neg_max2 = sb("neg_max2", [P, R])
        bias2 = sb("bias2", [P, R])
        sums2 = sb("sums2", [P, R])
        recip2 = sb("recip2", [P, R])
        row_scale = sb("row_scale", [P, R])
        p2 = sb("p2", [P, R, NT])
        p2T = sb("p2T", [P, R, NT])
        o2T = sb("o2T", [2 * D, NT])
        h2 = [sb(f"h2_{i}", [P, R, D]) for i in range(BUFS)]
        xc3 = sb("xc3", [P, R, D])
        sq3 = sb("sq3", [P, R, D])
        xn3 = sb("xn3", [P, R, D])
        st3 = sb("st3", [P, 5, R])

        x3_rows = sb("x3_rows", [128, NT])
        one_hotT = sb("one_hotT", [3 * EXPERTS, NT], BF16)
        top = sb("top", [P, R])
        top_rank = sb("top_rank", [P, R, EXPERTS])
        best_rank = sb("best_rank", [P, R])
        one_hot = sb("one_hot", [P, R, 4, EXPERTS], BF16)
        hidden = sb("hidden", [128, CHUNKS, NT])
        y_sb = sb("y_sb", [P, R, D])

        consts_loaded = sem("consts_loaded")
        rows_set = sem("rows_set")
        zeros_set = sem("zeros_set")
        id16_ready = sem("id16_ready")
        b2_step = sem("b2_step")
        a2_ready, a2_taken = sem("a2_ready"), sem("a2_taken")
        x_loaded = sem("x_loaded")
        parts_stored = sem("parts_stored")
        stacks_loaded = sem("stacks_loaded")
        shift_stored = sems("shift_stored", SIDES)
        shift_loaded = sems("shift_loaded", SIDES)
        y_stored = sem("y_stored")

        def norm_sems(i):
            names = ("summed", "mean", "centered", "squared", "sumsq", "var", "rstd", "normed")
            return {n: sem(f"ln{i}_{n}") for n in names}

        ln1, ln2, ln3 = norm_sems(1), norm_sems(2), norm_sems(3)
        xT_kv_ready, xT_kv_taken = sem("xT_kv_ready"), sem("xT_kv_taken")
        xT_q_ready, xT_q_taken = sem("xT_q_ready"), sem("xT_q_taken")
        z_ready, z_high, z_rest_ready, z_mid, z_low = [sem(f"z_{n}") for n in ("ready", "high", "rest", "mid", "low")]
        v_ready, v_taken = sem("v_ready"), sem("v_taken")
        max_scores, max_done = sems("max_scores", HEADS), sems("max_done", HEADS)
        exp_scores, exp_done = sems("exp_scores", HEADS), sems("exp_done", HEADS)
        sh_high, sh_rest1, sh_mid, sh_low = [sems(f"sh_{n}", SIDES) for n in ("high", "rest", "mid", "low")]
        shT_ready, shT_taken = sems("shT_ready", SIDES), sems("shT_taken", SIDES)
        pv_done = sems("pv_done", 4)
        o_taken = sems("o_taken", SIDES)
        oT_ready = sems("oT_ready", SIDES)
        o_recip, o_normed = sems("o_recip", SIDES), sems("o_normed", SIDES)
        o_summed = sem("o_summed")
        onT_ready, onT_taken = sem("onT_ready"), sem("onT_taken")
        h1_ready, h1_taken, h1b_ready = sem("h1_ready"), sem("h1_taken"), sem("h1b_ready")
        x2T_ready, x2T_taken = sem("x2T_ready"), sem("x2T_taken")
        qk2_ready, qk2_taken = sem("qk2_ready"), sem("qk2_taken")
        v2_ready, v2_taken, nonzero_ready, mask_ready = [sem(n) for n in ("v2_ready", "v2_taken", "nonzero_ready", "mask_ready")]
        scores2_ready, max2_ready, bias2_ready, exp2_done = [sem(n) for n in ("scores2_ready", "max2_ready", "bias2_ready", "exp2_done")]
        p2T_ready, p2T_taken = sem("p2T_ready"), sem("p2T_taken")
        o2_ready, o2_taken = sem("o2_ready"), sem("o2_taken")
        recip2_ready, scale2_ready = sem("recip2_ready"), sem("scale2_ready")
        out2_ready, h2_ready = sem("out2_ready"), sem("h2_ready")
        x3T_ready, x3T_taken = sem("x3T_ready"), sem("x3T_taken")
        logits_ready, top_ready = sem("logits_ready"), sem("top_ready")
        rank_ready, best_ready, one_hot_ready = sem("rank_ready"), sem("best_ready"), sem("one_hot_ready")
        ohT_ready, ohT_taken = sem("ohT_ready"), sem("ohT_taken")
        hid_ready, relu_done = sems("hid_ready", 2), sems("relu_done", 2)
        out_ready, y_ready = sem("out_ready"), sem("y_ready")

        N_CONST_DMAS = 10 + BUFS * 2
        PARTS_DMAS, STACK_DMAS, SHIFT_LOADS = 3, 12, 2

        def wait(eng, semaphore, value):
            if isinstance(value, int) and value <= 0:
                return
            eng.wait_ge(semaphore, value)

        def unit_count(u, b):
            return b * SIDES + u // HEADS + 1

        def before(u, by):
            return (u - by) % UNITS, (u - by) // UNITS

        def batches(t, live):
            return [t - i for i in range(DEPTH)], lambda s: s in live

        def run(iteration, loop):
            fill = DEPTH - 1
            trips = (BATCH - fill) // BUFS
            for t in range(fill):
                iteration(t, t % BUFS, STAGES[:t + 1])
            with loop(fill, fill + trips * BUFS - (BUFS - 1), BUFS) as t:
                for k in range(BUFS):
                    iteration(t + k, k, STAGES)
            for t in range(fill + trips * BUFS, BATCH + fill):
                live = "".join(s for i, s in enumerate(STAGES) if 0 <= t - i < BATCH)
                iteration(t, t % BUFS, live)

        def weight(name):
            lo, hi = COLS[name]
            return w_sb[:, lo:hi]

        block = ctx.enter_context(nc.Block())

        @block.sync
        def _(sp):
            xs = x.rearrange("n (s p r) d -> n p s r d", s=3, r=R)
            ys = out.rearrange("n (p r) d -> n p r d", r=R)
            q_rows = q_parts.rearrange("a (i m g) c -> m (a i) g c", m=2, g=PAIRS)
            k_rows = k_parts.rearrange("s a (i m g) c -> m (a i) s g c", m=2, g=PAIRS)
            TERMS = ((0, 0, 24, 0), (24, 0, 16, 8), (40, 0, 8, 16))

            def shift_io(side, batch, k):
                wait(sp, shT_taken[side], batch + 1)
                sp.dma_start(shift_parts[side].rearrange("m a g c -> (m a g) c"),
                             sh_rows[:, side, :]).then_inc(shift_stored[side], 16)
                wait(sp, shift_stored[side], batch * 16 + 16)
                for par in range(2):
                    row = 64 * par + SHIFT + 3 * side
                    sp.dma_start(q_stack[k][row:row + 3], shift_parts[side, par]).then_inc(shift_loaded[side], 16)

            def load_x(n):
                sp.dma_start(x_in[:].rearrange("p (s r) d -> p s r d", r=R),
                             xs[n] if isinstance(n, int) else xs[bass.ds(n, 1)].squeeze(0)).then_inc(x_loaded, 16)

            load_x(0)
            for dst, src in ((w_sb[:], w65), (gb_sb[:], ln_gb), (w1_sb[:], w1aug),
                             (w2_sb[:], w2.rearrange("(c p) d -> p c d", p=128)), (b2_rep[:], b2),
                             (qk2_w_sb[:], qk2_w.rearrange("c (i j) -> c i j", i=2)), (o2_w_sb[:], o2_w),
                             (bo2_sb[:], bo2.to_broadcast([P, D])), (id32[:], ident),
                             (rank_sb[:], expert_rank.to_broadcast([P, EXPERTS]))):
                sp.dma_start(dst, src).then_inc(consts_loaded, 16)
            for i in range(BUFS):
                for par in range(2):
                    sp.dma_start(k_stack[i][64 * par + SHIFT:64 * par + KROWS], shift_rows).then_inc(consts_loaded, 16)

            def iteration(t, k, live):
                (n, a, b, c, d, e, f), on = batches(t, live)
                if on("C"):
                    shift_io(1, c, (k - 3) % BUFS)
                if on("A"):
                    ka = (k - 1) % BUFS
                    wait(sp, z_low, a + 1)
                    sp.dma_start(q_parts.rearrange("a r c -> r a c"), z_parts[0:D, 0:3, :]).then_inc(parts_stored, 16)
                    for side in range(SIDES):
                        sp.dma_start(k_parts[side].rearrange("a r c -> r a c"),
                                     z_parts[D * side:D * side + D, 3:6, :]).then_inc(parts_stored, 16)
                    wait(sp, parts_stored, a * (16 * PARTS_DMAS) + 16 * PARTS_DMAS)
                    for first, q0, rows, k0 in TERMS:
                        for par in range(2):
                            at = 64 * par + first
                            sp.dma_start(q_stack[ka][at:at + rows],
                                         q_rows[par, q0:q0 + rows]).then_inc(stacks_loaded, 16)
                            sp.dma_start(k_stack[ka][at:at + rows],
                                         k_rows[par, k0:k0 + rows]).then_inc(stacks_loaded, 16)
                if on("N") and not (isinstance(n, int) and n + 1 == BATCH):
                    wait(sp, ln1["centered"], n + 1)
                    load_x(n + 1)
                if on("B"):
                    shift_io(0, b, (k - 2) % BUFS)
                if on("F"):
                    wait(sp, y_ready, f + 1)
                    sp.dma_start(ys[f] if isinstance(f, int) else ys[bass.ds(f, 1)].squeeze(0), y_sb[:]).then_inc(y_stored, 16)

            run(iteration, sp.Fori)
            sp.wait_ge(y_stored, 16 * BATCH)

        @block.tensor
        def _(pe):
            pe.wait_ge(consts_loaded, 16 * N_CONST_DMAS)
            pe.wait_ge(rows_set, 8)
            pe.wait_ge(zeros_set, 2 + BUFS)
            pe.wait_ge(id16_ready, 1)

            pe.matmul(m2[0:D + 1, 0:D + 1], qk2_w_sb[:, 1, :], qk2_w_sb[:, 0, :], start=True, stop=True).then_inc(a2_ready, 1)
            pe.wait_ge(a2_taken, 1)

            def max_unit(u, b, k):
                side, head = u // HEADS, u % HEADS
                at = 64 * (head % 2)
                if u == 0:
                    pe.wait_ge(stacks_loaded, b * (16 * STACK_DMAS) + 16 * STACK_DMAS)
                prior, back = before(u, 2)
                wait(pe, max_done[prior % HEADS], unit_count(prior, b + back))
                for r in range(R):
                    last = pe.matmul(max_bank[u % 2][0:P, r * NT:(r + 1) * NT],
                                     q_stack[k][at:at + SHIFT, head // 2, r * P:(r + 1) * P],
                                     k_stack[k][at:at + SHIFT, side, head // 2, :], start=True, stop=True)
                last.then_inc(max_scores[head], 1)

            def exp_unit(u, c, k):
                side, head = u // HEADS, u % HEADS
                at = 64 * (head % 2)
                rows = SHIFT + 3 * (side + 1)
                if u % HEADS == 0:
                    pe.wait_ge(shift_loaded[side], c * (16 * SHIFT_LOADS) + 16 * SHIFT_LOADS)
                prior, back = before(u, 2)
                wait(pe, exp_done[prior % HEADS], unit_count(prior, c + back))
                for kt in range(R):
                    last = pe.matmul(exp_bank[u % 2][0:P, kt * NT:(kt + 1) * NT],
                                     k_stack[k][at:at + rows, side, head // 2, kt * P:(kt + 1) * P],
                                     q_stack[k][at:at + rows, head // 2, :], start=True, stop=True)
                last.then_inc(exp_scores[head], 1)

            def pv(g, kt, c, k):
                side, half = g // 2, g % 2
                if kt == 0:
                    wait(pe, exp_done[(4 * g + 3) % HEADS], unit_count(4 * g + 3, c))
                if kt == 0 and g == 0:
                    wait(pe, v_taken, c + 1)
                    wait(pe, o_taken[1], c)
                if kt == 0 and g == 2:
                    wait(pe, o_taken[0], c + 1)
                for j in range(4):
                    head = 4 * half + j
                    last = pe.matmul(o_bank[32 * j:32 * j + 32, half * NT:(half + 1) * NT],
                                     v_aug[k][:, side * R + kt, head, :], probs[:, head, kt, :],
                                     start=(kt == 0), stop=(kt == R - 1), skip_group_check=True)
                if kt == R - 1:
                    last.then_inc(pv_done[g], 1)

            def transpose_tiles(dst, src, n):
                pe.transpose(dst[0:2 * D, 0:P], src[:, 0:2, :].rearrange("p r c -> p (r c)"), id32[0:P, 0:P])
                for r in range(1, n):
                    last = pe.transpose(dst[0:D, r * P:(r + 1) * P], src[:, r, :], id32[0:P, 0:P])
                return last

            def iteration(t, k, live):
                (n, a, b, c, d, e, f), on = batches(t, live)
                kb, kc, kd = (k - 2) % BUFS, (k - 3) % BUFS, (k - 4) % BUFS
                for slot in range(UNITS):
                    if on("C"):
                        exp_unit(slot, c, kc)
                    if on("B"):
                        max_unit(slot, b, kb)
                    if slot == 0 and on("A"):
                        wait(pe, xT_kv_taken, a + 1)
                        wait(pe, xT_q_taken, a + 1)
                        wait(pe, y_ready, f)
                        wait(pe, v_taken, a)
                        for i, (w, section) in enumerate((("q1", 0), ("q1", 0), ("k1", 1), ("k1", 2))):
                            half = i % 2
                            last = pe.matmul(m0[D * half:D * half + D, (i // 2) * NT:(i // 2 + 1) * NT],
                                             weight(w), x1T[:, section, :], start=True, stop=True,
                                             skip_group_check=True)
                        last.then_inc(z_ready, 1)
                    if slot == 1:
                        if on("C"):
                            wait(pe, sh_low[1], c + 1)
                            wait(pe, shT_taken[0], c + 1)
                            if on("A"):
                                wait(pe, xT_kv_taken, a + 1)
                            if on("E"):
                                wait(pe, x2T_taken, e + 1)
                            shift_turn(1)
                        if on("E"):
                            wait(pe, x2T_taken, e + 1)
                            wait(pe, h2_ready, e)
                            if on("A"):
                                wait(pe, xT_q_taken, a + 1)
                            pe.matmul(m2[0:D + 1, 0:NT], a2_sb[:], x2T[:], start=True, stop=True).then_inc(qk2_ready, 1)
                    if slot == 2 and on("F"):
                        wait(pe, ln3["normed"], f + 1)
                        wait(pe, y_ready, f)
                        if on("A"):
                            wait(pe, z_rest_ready, a + 1)
                        transpose_tiles(m0, xn3, R).then_inc(x3T_ready, 1)
                    if slot == 3:
                        if on("D"):
                            wait(pe, o_taken[0], d + 1)
                            if on("C"):
                                wait(pe, shT_taken[1], c + 1)
                            if on("E"):
                                wait(pe, x2T_taken, e + 1)
                            output_turn(0)
                        if on("E"):
                            wait(pe, qk2_taken, e + 1)
                            for r in range(R):
                                last = pe.matmul(m2[0:P, r * (D + 2):(r + 1) * (D + 2)], x2T[:, r * P:(r + 1) * P],
                                                 weight("v2"), start=True, stop=True)
                            last.then_inc(v2_ready, 1)
                    if slot in (2, 3) and on("D"):
                        pv(3, slot - 2, d, kd)
                    if slot == 4 and on("A"):
                        wait(pe, z_rest_ready, a + 1)
                        if on("F"):
                            wait(pe, x3T_taken, f + 1)
                        for j in range(SIDES * R):
                            last = pe.matmul(m0[0:P, j * D:(j + 1) * D], x1T[:, 1 + j // R, (j % R) * P:(j % R + 1) * P],
                                             weight("v1"), start=True, stop=True)
                        last.then_inc(v_ready, 1)
                    if slot == 5 and on("F"):
                        wait(pe, x3T_taken, f + 1)
                        if on("A"):
                            wait(pe, v_taken, a + 1)
                        for r in range(R):
                            last = pe.matmul(m0[0:P, r * EXPERTS:(r + 1) * EXPERTS], x3_rows[0:D + 1, r * P:(r + 1) * P],
                                             weight("router"), start=True, stop=True)
                        last.then_inc(logits_ready, 1)
                    if slot == 5:
                        if on("D"):
                            wait(pe, o_taken[1], d + 1)
                            wait(pe, o_normed[0], d + 1)
                            output_turn(1)
                        if on("E"):
                            wait(pe, v2_taken, e + 1)
                            wait(pe, nonzero_ready, e + 1)
                            for r in range(R):
                                last = pe.matmul(m2[0:P, r * NT:(r + 1) * NT], x2T[:, r * P:(r + 1) * P],
                                                 qk2[:], start=True, stop=True)
                            last.then_inc(scores2_ready, 1)
                    if slot in (6, 7) and on("C"):
                        pv(0, slot - 6, c, kc)
                    if slot == 7 and on("D"):
                        wait(pe, o_summed, d + 1)
                        transpose_tiles(m1, on_sum, R).then_inc(onT_ready, 1)
                    if slot == 8:
                        if on("F"):
                            wait(pe, one_hot_ready, f + 1)
                            for r in range(R):
                                last = pe.matmul(m0[:, r * P:(r + 1) * P],
                                                 one_hot[:, r].rearrange("p i e -> p (i e)"), id16[0:P, 0:P],
                                                 start=True, stop=True)
                            last.then_inc(ohT_ready, 1)
                        if on("E"):
                            wait(pe, exp2_done, e + 1)
                            for kt in range(R):
                                for r in range(R):
                                    last = pe.transpose(m2[0:P, kt * NT + r * P:kt * NT + (r + 1) * P],
                                                        p2[:, r, kt * P:(kt + 1) * P], id32[0:P, 0:P])
                            last.then_inc(p2T_ready, 1)
                    if slot in (9, 11) and on("C"):
                        pv(1, (slot - 9) // 2, c, kc)
                    if slot == 9 and on("B"):
                        wait(pe, sh_low[0], b + 1)
                        if on("C"):
                            wait(pe, shT_taken[1], c + 1)
                        if on("D"):
                            wait(pe, onT_taken, d + 1)
                        shift_turn(0)
                    if slot == 10:
                        if on("F"):
                            wait(pe, ohT_taken, f + 1)
                            expert_in(0)
                        if on("E"):
                            wait(pe, p2T_taken, e + 1)
                            for kt in range(R):
                                last = pe.matmul(m2[D * kt:D * kt + D, 0:NT], v2_sb[:, kt, :], p2T[:, kt, :],
                                                 start=True, stop=True, skip_group_check=True)
                            last.then_inc(o2_ready, 1)
                        if on("D"):
                            wait(pe, onT_taken, d + 1)
                            if on("B"):
                                wait(pe, shT_taken[0], b + 1)
                            for r in range(R):
                                last = pe.matmul(m1[0:P, r * D:(r + 1) * D], onT[:, r * P:(r + 1) * P], weight("o1"),
                                                 start=True, stop=True)
                            last.then_inc(h1_ready, 1)
                    if slot == 12:
                        if on("F"):
                            wait(pe, relu_done[0], f + 1)
                            expert_in(1)
                        if on("E"):
                            wait(pe, o2_taken, e + 1)
                            for r in range(R):
                                last = pe.matmul(m2[0:P, r * D:(r + 1) * D], o2T[:, r * P:(r + 1) * P],
                                                 o2_w_sb[:], start=True, stop=True)
                            last.then_inc(out2_ready, 1)
                    if slot == 13 and on("N"):
                        wait(pe, ln1["normed"], n + 1)
                        wait(pe, xT_kv_taken, n)
                        if on("B"):
                            wait(pe, shT_taken[0], b + 1)
                        if on("D"):
                            wait(pe, h1_taken, d + 1)
                        transpose_tiles(m1, xn1[:, R:3 * R, :], 2 * R).then_inc(xT_kv_ready, 1)
                    if slot in (13, 15) and on("C"):
                        pv(2, (slot - 13) // 2, c, kc)
                    if slot == 14:
                        if on("N"):
                            wait(pe, xT_q_taken, n)
                            if on("E"):
                                wait(pe, h2_ready, e + 1)
                            transpose_tiles(m2, xn1[:, 0:R, :], R).then_inc(xT_q_ready, 1)
                        if on("F"):
                            wait(pe, relu_done[1], f + 1)
                            for r in range(R):
                                for ch in range(CHUNKS):
                                    pe.matmul(m0[0:P, r * D:(r + 1) * D], hidden[:, ch, r * P:(r + 1) * P], w2_sb[:, ch, :],
                                              start=(ch == 0), stop=False)
                                last = pe.matmul(m0[0:P, r * D:(r + 1) * D], one_hotT[:, r * P:(r + 1) * P], b2_parts[:],
                                                 start=False, stop=True)
                            last.then_inc(out_ready, 1)
                    if slot == 15 and on("D"):
                        wait(pe, ln2["normed"], d + 1)
                        if on("B"):
                            wait(pe, shT_taken[0], b + 1)
                        if on("N"):
                            wait(pe, xT_kv_taken, n + 1)
                        transpose_tiles(m1, xn2, R).then_inc(x2T_ready, 1)

            def shift_turn(side):
                for r in range(R):
                    last = pe.matmul(m1[0:2 * 3 * PAIRS, r * P:(r + 1) * P],
                                     sh_parts[:, side, r].rearrange("p m a g -> p (m a g)"), id16[0:P, 0:P],
                                     start=True, stop=True)
                last.then_inc(shT_ready[side], 1)

            def output_turn(side):
                for half in range(2):
                    for r in range(R):
                        at = (half * R + r) * 128
                        last = pe.transpose(m1[0:P, at:at + 128], o_sb[:, side, half, r * P:(r + 1) * P], id32[:])
                last.then_inc(oT_ready[side], 1)

            def expert_in(i):
                for ch in range(2):
                    at = (2 * i + ch) * 128
                    last = pe.matmul(m0[:, ch * NT:(ch + 1) * NT], w1_sb[:, at:at + 128], x3_rows[:], start=True, stop=True)
                last.then_inc(hid_ready[i], 1)

            run(iteration, pe.Fori)

        @block.scalar
        def _(act):
            act.wait_ge(consts_loaded, 16 * N_CONST_DMAS)
            act.wait_ge(rows_set, 8)
            act.wait_ge(zeros_set, 2 + BUFS)

            act.wait_ge(a2_ready, 1)
            act.copy(a2_sb[:], m2[0:D + 1, 0:D + 1]).then_inc(a2_taken, 1)

            def exp_unit(u, c):
                wait(act, exp_scores[u % HEADS], unit_count(u, c))
                if u % 4 == 0:
                    g = u // 4
                    wait(act, pv_done[(g + 2) % 4], c if g < 2 else c + 1)
                act.activation(probs[:, u % HEADS].rearrange("p k q -> p (k q)"), exp_bank[u % 2][0:P, 0:R * NT],
                               ACT.Exp, scale=SCALE).then_inc(exp_done[u % HEADS], 1)

            def shift_take(side, batch):
                wait(act, shT_ready[side], batch + 1)
                wait(act, shift_stored[side], batch * 16)
                act.copy(sh_rows[:, side, :], m1[0:2 * 3 * PAIRS, 0:NT]).then_inc(shT_taken[side], 1)

            def output_take(side, batch):
                wait(act, pv_done[2 * side + 1], batch + 1)
                wait(act, oT_ready[side], batch)
                act.copy(o_sb[:, side].rearrange("p h q -> p (h q)"), o_bank[:, 0:2 * NT]).then_inc(o_taken[side], 1)

            def iteration(t, k, live):
                (n, a, b, c, d, e, f), on = batches(t, live)
                for slot in range(UNITS):
                    if on("C"):
                        exp_unit(slot, c)
                    if slot == 0 and on("A"):
                        wait(act, z_ready, a + 1)
                        wait(act, parts_stored, a * (16 * PARTS_DMAS))
                        act.copy(z_parts[:, 0:6:5, :], m0[:, 0:2 * NT].rearrange("p (i c) -> p i c", i=2)).then_inc(z_high, 1)
                    if slot == 1:
                        if on("C"):
                            shift_take(1, c)
                        if on("E"):
                            wait(act, qk2_ready, e + 1)
                            wait(act, scores2_ready, e)
                            act.copy(qk2[:], m2[0:D + 1, 0:NT]).then_inc(qk2_taken, 1)
                    if slot == 2 and on("F"):
                        wait(act, x3T_ready, f + 1)
                        wait(act, hid_ready[1], f)
                        act.copy(x3_rows[0:D], m0[0:D, 0:NT]).then_inc(x3T_taken, 1)
                    if slot == 3 and on("D"):
                        output_take(1, d)
                    if slot == 4 and on("A"):
                        wait(act, v_ready, a + 1)
                        wait(act, pv_done[3], a - 2)
                        act.copy(v_aug[(k - 1) % BUFS][:, :, :, 0:DH],
                                 m0[0:P, 0:SIDES * R * D].rearrange("p (j h d) -> p j h d", h=HEADS, d=DH)
                                 ).then_inc(v_taken, 1)
                    if slot == 6 and on("E"):
                        wait(act, bias2_ready, e + 1)
                        wait(act, p2T_ready, e)
                        wait(act, recip2_ready, e)
                        for r in range(R):
                            last = act.activation(p2[:, r, :], m2[0:P, r * NT:(r + 1) * NT], ACT.Exp,
                                                  bias=bias2[:, r:r + 1], scale=SCALE, accum_out=sums2[:, r:r + 1])
                        last.then_inc(exp2_done, 1)
                    if slot == 7 and on("D"):
                        wait(act, onT_ready, d + 1)
                        wait(act, h1_ready, d)
                        act.copy(onT[0:D], m1[0:D, 0:NT]).then_inc(onT_taken, 1)
                    if slot == 8 and on("F"):
                        wait(act, ohT_ready, f + 1)
                        wait(act, out_ready, f)
                        act.copy(one_hotT[:], m0[0:3 * EXPERTS, 0:NT])
                        act.activation(x3_rows[96:128], m0[96:128, 0:NT], ACT.Copy, bias=-1.0).then_inc(ohT_taken, 1)
                    if slot == 8 and on("E"):
                        wait(act, p2T_ready, e + 1)
                        wait(act, o2_ready, e)
                        act.copy(p2T[:].rearrange("p k q -> p (k q)"), m2[0:P, 0:R * NT]).then_inc(p2T_taken, 1)
                    if slot == 9 and on("B"):
                        shift_take(0, b)
                    if slot == 10:
                        if on("F"):
                            expert_relu(0, f)
                        if on("E"):
                            wait(act, o2_ready, e + 1)
                            wait(act, out2_ready, e)
                            act.copy(o2T[:], m2[:, 0:NT]).then_inc(o2_taken, 1)
                    if slot == 11 and on("C"):
                        output_take(0, c)
                    if slot == 12 and on("F"):
                        expert_relu(1, f)
                    if slot == 13 and on("N"):
                        wait(act, xT_kv_ready, n + 1)
                        wait(act, v_ready, n)
                        act.activation(x1T[0:D, 1:3].rearrange("p s c -> p (s c)"), m1[0:D, 0:2 * NT], ACT.Identity,
                                       bias=gb_sb[:, 1:2], scale=gb_sb[:, 0:1]).then_inc(xT_kv_taken, 1)
                    if slot == 14 and on("N"):
                        wait(act, xT_q_ready, n + 1)
                        act.activation(x1T[0:D, 0], m2[0:D, 0:NT], ACT.Identity,
                                       bias=gb_sb[:, 1:2], scale=gb_sb[:, 0:1]).then_inc(xT_q_taken, 1)
                    if slot == 15 and on("D"):
                        wait(act, x2T_ready, d + 1)
                        wait(act, scores2_ready, d)
                        act.copy(x2T[0:D], m1[0:D, 0:NT]).then_inc(x2T_taken, 1)

            def expert_relu(i, f):
                wait(act, hid_ready[i], f + 1)
                wait(act, out_ready, f)
                act.activation(hidden[:, 2 * i:2 * i + 2].rearrange("p h c -> p (h c)"), m0[:, 0:2 * NT],
                               ACT.Relu).then_inc(relu_done[i], 1)

            run(iteration, act.Fori)

        @block.vector
        def _(dve):
            dve.memset(x1T[D:D + 1], 1.0).then_inc(rows_set, 1)
            dve.memset(onT[D:D + 1], 2.0).then_inc(rows_set, 1)
            dve.memset(minus_half[:], -0.5).then_inc(zeros_set, 1)
            dve.memset(x2T[D:D + 1], 1.0).then_inc(rows_set, 1)
            dve.memset(x3_rows[64:96], 1.0).then_inc(rows_set, 1)
            dve.memset(h1[:], 0.0).then_inc(zeros_set, 1)
            for i in range(BUFS):
                dve.memset(v_aug[i][:], 0.0).then_inc(zeros_set, 1)
            dve.wait_ge(zeros_set, 2 + BUFS)
            for i in range(BUFS):
                dve.memset(v_aug[i][:, :, :, DH:DH + 1], 1.0).then_inc(rows_set, 1)
            dve.wait_ge(consts_loaded, 16 * N_CONST_DMAS)
            dve.tensor_copy(id16[:], id32[:]).then_inc(id16_ready, 1)
            dve.tensor_copy(b2_parts[:], b2_rep[:]).then_inc(b2_step, 1)
            dve.wait_ge(b2_step, 1)
            dve.tensor_tensor(b2_rest[:], b2_rep[:], b2_parts[:], ALU.subtract).then_inc(b2_step, 1)
            dve.wait_ge(b2_step, 2)
            dve.tensor_copy(b2_mid[:], b2_rest[:]).then_inc(b2_step, 1)
            dve.wait_ge(b2_step, 3)
            dve.tensor_copy(b2_parts[EXPERTS:2 * EXPERTS], b2_mid[EXPERTS:2 * EXPERTS])
            dve.tensor_tensor(b2_parts[2 * EXPERTS:], b2_rest[2 * EXPERTS:], b2_mid[2 * EXPERTS:],
                              ALU.subtract).then_inc(rows_set, 1)

            def norm_sum(ln, src, st, b):
                wait(dve, ln["centered"], b)
                dve.reduce_sum(st[:, 0], src, axis=AX_X).then_inc(ln["summed"], 1)
                dve.wait_ge(ln["summed"], b + 1)
                dve.tensor_scalar(st[:, 1], st[:, 0], -1.0 / D, None, ALU.mult).then_inc(ln["mean"], 1)

            def norm_var(ln, sq, st, b):
                dve.wait_ge(ln["squared"], b + 1)
                wait(dve, ln["normed"], b)
                dve.reduce_sum(st[:, 2], sq[:], axis=AX_X).then_inc(ln["sumsq"], 1)
                dve.wait_ge(ln["sumsq"], b + 1)
                dve.tensor_scalar(st[:, 3], st[:, 2], 1.0 / D, LN_EPS, ALU.mult, ALU.add).then_inc(ln["var"], 1)

            def max_unit(u, b):
                side, head = u // HEADS, u % HEADS
                at = (head % 2) * PAIRS + head // 2
                dve.wait_ge(max_scores[head], unit_count(u, b))
                dve.tensor_reduce(neg_max[:, side, :, at], max_bank[u % 2][0:P, 0:R * NT].rearrange("p (r c) -> p r c", r=R),
                                  AX_X, ALU.max, negate=True).then_inc(max_done[head], 1)

            def shift_split(side, b):
                nm = neg_max[:, side].rearrange("p r (m g) -> p r m g", g=PAIRS)
                rest = sh_rest[:, side].rearrange("p r (m g) -> p r m g", g=PAIRS)
                high, mid, low = [sh_parts[:, side, :, :, i, :] for i in range(3)]
                dve.wait_ge(max_done[HEADS - 1], unit_count(side * HEADS + HEADS - 1, b))
                wait(dve, shT_ready[side], b)
                dve.tensor_copy(high, nm).then_inc(sh_high[side], 1)
                dve.wait_ge(sh_high[side], b + 1)
                dve.tensor_tensor(rest, nm, high, ALU.subtract).then_inc(sh_rest1[side], 1)
                dve.wait_ge(sh_rest1[side], b + 1)
                dve.tensor_copy(mid, rest).then_inc(sh_mid[side], 1)
                dve.wait_ge(sh_mid[side], b + 1)
                dve.tensor_tensor(low, rest, mid, ALU.subtract).then_inc(sh_low[side], 1)

            def output_recip(side, d):
                dve.wait_ge(oT_ready[side], d + 1)
                dve.reciprocal(recip1[:, side].rearrange("p h r j -> p (h r j)"),
                               m1[0:P, :].rearrange("p (n q) -> p n q", q=32)[:, :, DH]).then_inc(o_recip[side], 1)

            def output_scale(side, d):
                o = m1[0:P, :].rearrange("p (h r j q) -> p h r j q", h=2, r=R, q=32)
                dve.wait_ge(o_recip[side], d + 1)
                for half in range(2):
                    last = dve.tensor_tensor(on_side[:, side, :, half], o[:, half, :, :, 0:DH],
                                             recip1[:, side, half].unsqueeze(3).to_broadcast([P, R, 4, DH]), ALU.mult)
                last.then_inc(o_normed[side], 1)

            def iteration(t, k, live):
                (n, a, b, c, d, e, f), on = batches(t, live)
                for slot in range(UNITS):
                    if slot == 0 and on("C"):
                        shift_split(1, c)
                    if slot == 8 and on("B"):
                        shift_split(0, b)
                    if on("B"):
                        max_unit(slot, b)
                    if slot == 0 and on("A"):
                        z = m0[:, 0:2 * NT].rearrange("p (i c) -> p i c", i=2)
                        dve.wait_ge(z_high, a + 1)
                        wait(dve, z_low, a)
                        dve.tensor_tensor(z_rest[:], z, z_parts[:, 0:6:5, :], ALU.subtract).then_inc(z_rest_ready, 1)
                        dve.wait_ge(z_rest_ready, a + 1)
                        dve.tensor_copy(z_parts[:, 1:5:3, :], z_rest[:]).then_inc(z_mid, 1)
                    if slot == 1 and on("N"):
                        dve.wait_ge(x_loaded, n * 16 + 16)
                        norm_sum(ln1, x_in[:], st1, n)
                    if slot == 4 and on("N"):
                        norm_var(ln1, sq1, st1, n)
                    if slot == 3:
                        v2 = m2[0:P, 0:R * (D + 2)].rearrange("p (r c) -> p r c", r=R)
                        if on("D"):
                            output_recip(0, d)
                        if on("E"):
                            dve.wait_ge(v2_ready, e + 1)
                            dve.tensor_scalar(nonzero[:], v2[:, :, D:D + 2], 0.0, None, ALU.not_equal).then_inc(nonzero_ready, 1)
                        if on("D"):
                            output_scale(0, d)
                        if on("E"):
                            wait(dve, o2_ready, e)
                            dve.tensor_copy(v2_sb[:], v2[:, :, 0:D]).then_inc(v2_taken, 1)
                            dve.wait_ge(nonzero_ready, e + 1)
                            dve.tensor_tensor(row_mask[:], nonzero[:, :, 0], nonzero[:, :, 1], ALU.mult).then_inc(mask_ready, 1)
                    if slot == 5:
                        if on("F"):
                            route_top(f)
                        if on("D"):
                            output_recip(1, d)
                        if on("F"):
                            route_rank(f)
                        if on("D"):
                            output_scale(1, d)
                        if on("F"):
                            route_best(f)
                        if on("D"):
                            dve.wait_ge(o_normed[1], d + 1)
                            wait(dve, onT_ready, d)
                            s0, s1 = [on_side[:, s].rearrange("p r h j q -> p (r h j q)") for s in range(SIDES)]
                            dve.tensor_tensor(on_sum[:].rearrange("p r c -> p (r c)"), s0, s1, ALU.add).then_inc(o_summed, 1)
                        if on("F"):
                            route_one_hot(f)
                        if on("E"):
                            dve.wait_ge(scores2_ready, e + 1)
                            dve.tensor_reduce(neg_max2[:], m2[0:P, 0:R * NT].rearrange("p (r c) -> p r c", r=R), AX_X,
                                              ALU.max, negate=True).then_inc(max2_ready, 1)
                            dve.wait_ge(max2_ready, e + 1)
                            wait(dve, exp2_done, e)
                            dve.tensor_scalar(bias2[:], neg_max2[:], SCALE, None, ALU.mult).then_inc(bias2_ready, 1)
                    if slot == 8 and on("E"):
                        dve.wait_ge(exp2_done, e + 1)
                        dve.reciprocal(recip2[:], sums2[:]).then_inc(recip2_ready, 1)
                        dve.wait_ge(recip2_ready, e + 1)
                        dve.wait_ge(mask_ready, e + 1)
                        dve.tensor_tensor(row_scale[:], recip2[:], row_mask[:], ALU.mult).then_inc(scale2_ready, 1)
                    if slot == 10 and on("D"):
                        dve.wait_ge(h1_ready, d + 1)
                        wait(dve, ln2["centered"], d)
                        wait(dve, h1b_ready, d)
                        dve.tensor_copy(h1[:].rearrange("p r c -> p (r c)"), m1[0:P, 0:R * D]).then_inc(h1_taken, 1)
                        dve.wait_ge(h1_taken, d + 1)
                        norm_sum(ln2, h1[:], st2, d)
                    if slot == 12 and on("D"):
                        norm_var(ln2, sq2, st2, d)
                    if slot == 12 and on("E"):
                        ke = (k - 5) % BUFS
                        dve.wait_ge(out2_ready, e + 1)
                        dve.wait_ge(scale2_ready, e + 1)
                        dve.wait_ge(h1b_ready, e + 1)
                        for r in range(R):
                            last = dve.scalar_tensor_tensor(out=h2[ke][:, r, :], in0=m2[0:P, r * D:(r + 1) * D],
                                                            scalar=row_scale[:, r:r + 1], in1=h1b[ke][:, r, :],
                                                            op0=ALU.mult, op1=ALU.add)
                        last.then_inc(h2_ready, 1)
                        dve.wait_ge(h2_ready, e + 1)
                        norm_sum(ln3, h2[ke][:], st3, e)
                    if slot == 14 and on("E"):
                        norm_var(ln3, sq3, st3, e)
                    if slot == 14 and on("F"):
                        dve.wait_ge(out_ready, f + 1)
                        wait(dve, y_stored, f * 16)
                        dve.scalar_tensor_tensor(out=y_sb[:].rearrange("p r c -> p (r c)"), in0=m0[0:P, 0:R * D], scalar=0.0,
                                                 in1=h2[(k - 6) % BUFS][:].rearrange("p r c -> p (r c)"),
                                                 op0=ALU.max, op1=ALU.add).then_inc(y_ready, 1)

            def route_top(f):
                dve.wait_ge(logits_ready, f + 1)
                dve.reduce_max(top[:], m0[0:P, 0:R * EXPERTS].rearrange("p (r e) -> p r e", r=R),
                               axis=AX_X).then_inc(top_ready, 1)

            def route_rank(f):
                dve.wait_ge(top_ready, f + 1)
                for r in range(R):
                    last = dve.scalar_tensor_tensor(out=top_rank[:, r, :], in0=m0[0:P, r * EXPERTS:(r + 1) * EXPERTS],
                                                    scalar=top[:, r:r + 1], in1=rank_sb[:], op0=ALU.is_equal, op1=ALU.mult)
                last.then_inc(rank_ready, 1)

            def route_best(f):
                dve.wait_ge(rank_ready, f + 1)
                dve.reduce_max(best_rank[:], top_rank[:], axis=AX_X).then_inc(best_ready, 1)

            def route_one_hot(f):
                dve.wait_ge(best_ready, f + 1)
                wait(dve, ohT_ready, f)
                for r in range(R):
                    last = dve.tensor_scalar(one_hot[:, r], top_rank[:, r].unsqueeze(1).to_broadcast([P, 4, EXPERTS]),
                                             best_rank[:, r:r + 1], None, ALU.is_equal)
                last.then_inc(one_hot_ready, 1)

            run(iteration, dve.Fori)

        @block.gpsimd
        def _(pool):
            pool.wait_ge(consts_loaded, 16 * N_CONST_DMAS)
            pool.wait_ge(zeros_set, 2 + BUFS)

            def norm_center(ln, src, xc, sq, st, groups, b):
                pool.wait_ge(ln["mean"], b + 1)
                wait(pool, ln["normed"], b)
                pool.tensor_tensor(xc[:], src, st[:, 1].unsqueeze(2).to_broadcast([P, groups, D]),
                                   ALU.add).then_inc(ln["centered"], 1)
                pool.wait_ge(ln["centered"], b + 1)
                wait(pool, ln["sumsq"], b)
                pool.tensor_tensor(sq[:], xc[:], xc[:], ALU.mult).then_inc(ln["squared"], 1)

            def norm_scale(ln, xc, xn, st, groups, b, read):
                pool.wait_ge(ln["var"], b + 1)
                pool.tensor_tensor(st[:, 4], st[:, 3], minus_half[:].to_broadcast([P, groups]),
                                   ALU.pow).then_inc(ln["rstd"], 1)
                pool.wait_ge(ln["rstd"], b + 1)
                wait(pool, read, b)
                pool.tensor_tensor(xn[:], xc[:], st[:, 4].unsqueeze(2).to_broadcast([P, groups, D]),
                                   ALU.mult).then_inc(ln["normed"], 1)

            def iteration(t, k, live):
                (n, a, b, c, d, e, f), on = batches(t, live)
                if on("A"):
                    pool.wait_ge(z_mid, a + 1)
                    pool.tensor_tensor(z_parts[:, 2:4, :], z_rest[:], z_parts[:, 1:5:3, :], ALU.subtract).then_inc(z_low, 1)
                if on("N"):
                    norm_center(ln1, x_in[:], xc1, sq1, st1, 3 * R, n)
                    norm_scale(ln1, xc1, xn1, st1, 3 * R, n, xT_q_ready)
                if on("D"):
                    pool.wait_ge(h1_taken, d + 1)
                    wait(pool, h2_ready, d - 2)
                    pool.tensor_tensor(h1b[(k - 4) % BUFS][:], h1[:], bo2_sb[:].unsqueeze(1).to_broadcast([P, R, D]),
                                       ALU.add).then_inc(h1b_ready, 1)
                    norm_center(ln2, h1[:], xc2, sq2, st2, R, d)
                    norm_scale(ln2, xc2, xn2, st2, R, d, x2T_ready)
                if on("E"):
                    norm_center(ln3, h2[(k - 5) % BUFS][:], xc3, sq3, st3, R, e)
                    norm_scale(ln3, xc3, xn3, st3, R, e, x3T_ready)

            run(iteration, pool.Fori)


def kernel(**inputs):
    import numpy as np
    import concourse.bacc as bacc
    from concourse.bass_utils import run_bass_kernel_spmd

    a = {name: np.asarray(value) for name, value in inputs.items()}

    def with_bias(w, b):
        return np.concatenate([w.T, b[None, :]], axis=0)

    def by_stack_row(w):
        return w.reshape(D + 1, PAIRS, 2, DH).transpose(0, 3, 2, 1).reshape(D + 1, D)

    q2 = with_bias(a["L0_attn_Wq"], a["L0_attn_bq"])
    k2 = with_bias(a["L0_attn_Wk"], a["L0_attn_bk"])
    w65 = np.concatenate([
        by_stack_row(with_bias(a["L0_tok_Wq"], a["L0_tok_bq"])),
        by_stack_row(with_bias(a["L0_tok_Wk"], a["L0_tok_bk"])),
        with_bias(a["L0_tok_Wv"], a["L0_tok_bv"]),
        with_bias(a["L0_tok_Wo"], a["L0_tok_bo"]),
        with_bias(a["L0_attn_Wv"], a["L0_attn_bv"]), q2[:, 0:1], k2[:, 0:1],
        with_bias(a["L0_ffn_router_w"], a["L0_ffn_router_b"]),
    ], axis=1)
    expand = np.kron(np.eye(EXPERTS, dtype=np.float32), np.full((1, HID), 2.0 ** 126, np.float32))
    w1 = a["L0_ffn_W1"].transpose(1, 0, 2).reshape(D, EXPERTS * HID)
    w1aug = np.concatenate([w1, a["L0_ffn_b1"].reshape(1, -1), np.zeros((31, EXPERTS * HID), np.float32), expand])
    shift_rows = np.zeros((3 * SIDES, SIDES, PAIRS, NT), np.float32)
    for side in range(SIDES):
        shift_rows[3 * side:3 * side + 3, side] = 1.0
    arrays = {
        "x": a["x"], "w65": w65, "ln_gb": np.stack([a["L0_tok_ln_g"], a["L0_tok_ln_b"]], axis=1),
        "w1aug": w1aug, "w2": a["L0_ffn_W2"].reshape(EXPERTS * HID, D), "b2": np.tile(a["L0_ffn_b2"], (3, 1)),
        "qk2_w": np.concatenate([a["L0_attn_Wq"], a["L0_attn_bq"][:, None], a["L0_attn_Wk"], a["L0_attn_bk"][:, None]], axis=1),
        "o2_w": np.tile(a["L0_attn_Wo"].T, (2, 1)),
        "bo2": a["L0_attn_bo"][None, :], "ident": np.eye(128, dtype=np.float32),
        "expert_rank": np.arange(EXPERTS, 0, -1, dtype=np.float32)[None, :],
        "shift_rows": shift_rows.astype(mybir.dt.np(BF16)),
    }
    arrays = {name: np.ascontiguousarray(v) for name, v in arrays.items()}
    nc = bacc.Bacc("TRN2", target_bir_lowering=False, num_devices=1)
    args = [nc.dram_tensor(name, v.shape, mybir.dt.from_np(v.dtype), kind="ExternalInput").ap()
            for name, v in arrays.items()]
    out = nc.dram_tensor("out", (BATCH, NT, D), F32, kind="ExternalOutput").ap()
    audio_tower_kernel(nc, *args, out)
    result = run_bass_kernel_spmd(nc, [arrays], core_ids=[0])
    return result.results[0]["out"]
```

```python
from contextlib import ExitStack

import concourse.bass as bass
from concourse import mybir
from concourse.alu_op_type import AluOpType as ALU

ACT = mybir.ActivationFunctionType
F32 = mybir.dt.float32
BF16 = mybir.dt.bfloat16
AX_X = mybir.AxisListType.X

BATCH = 64
P = 125
R = 2
NT = P * R
D = 64
HEADS = 8
DH = D // HEADS
SIDES = 2
UNITS = SIDES * HEADS
PAIRS = HEADS // 2
EXPERTS = 32
HID = 16
CHUNKS = EXPERTS * HID // 128
LN_EPS = 1e-5
SCALE = 0.125
SHIFT = 48
KROWS = SHIFT + 3 * SIDES
BUFS = 3
STAGES = "NABCDEF"
DEPTH = len(STAGES)

COLS = {}
_at = 0
for _name, _width in (("q1", D), ("k1", D), ("v1", D), ("o1", D), ("v2", D + 2),
                      ("router", EXPERTS)):
    COLS[_name] = (_at, _at + _width)
    _at += _width
W65_COLS = _at


def audio_tower_kernel(nc, x, w65, ln_gb, w1aug, w2, b2, qk2_w, o2_w, bo2, ident, expert_rank, shift_rows, out):
    with ExitStack() as ctx:
        def sb(name, shape, dt=F32):
            return ctx.enter_context(nc.sbuf_tensor(name, shape, dt))

        def bank(name):
            return ctx.enter_context(nc.psum_tensor(name, [128, 512], F32))

        def sem(name):
            return ctx.enter_context(nc.semaphore(name))

        def sems(name, n):
            return [sem(f"{name}{i}") for i in range(n)]

        q_parts = nc.dram_tensor("q_parts", (3, D, NT), BF16, kind="Internal").ap()
        k_parts = nc.dram_tensor("k_parts", (SIDES, 3, D, NT), BF16, kind="Internal").ap()
        shift_parts = nc.dram_tensor("shift_parts", (SIDES, 2, 3, PAIRS, NT), BF16, kind="Internal").ap()

        max_bank = [bank("max_bank0"), bank("max_bank1")]
        exp_bank = [bank("exp_bank0"), bank("exp_bank1")]
        o_bank = bank("o_bank")
        m0 = bank("m0")
        m1 = bank("m1")
        m2 = bank("m2")

        w_sb = sb("w_sb", [D + 1, W65_COLS])
        gb_sb = sb("gb_sb", [D, 2])
        w1_sb = sb("w1_sb", [128, EXPERTS * HID])
        w2_sb = sb("w2_sb", [128, CHUNKS, D])
        b2_rep = sb("b2_rep", [3 * EXPERTS, D])
        b2_rest = sb("b2_rest", [3 * EXPERTS, D])
        b2_mid = sb("b2_mid", [3 * EXPERTS, D], BF16)
        b2_parts = sb("b2_parts", [3 * EXPERTS, D], BF16)
        qk2_w_sb = sb("qk2_w_sb", [D, 2, D + 1])
        a2_sb = sb("a2_sb", [D + 1, D + 1])
        o2_w_sb = sb("o2_w_sb", [2 * D, D])
        bo2_sb = sb("bo2_sb", [P, D])
        id32 = sb("id32", [128, 128])
        id16 = sb("id16", [128, 128], BF16)
        id_twice = sb("id_twice", [2 * D, D])
        minus_half = sb("minus_half", [P, 1])
        rank_sb = sb("rank_sb", [P, EXPERTS])

        x_in = sb("x_in", [P, 3 * R, D])
        xc1 = sb("xc1", [P, 3 * R, D])
        sq1 = sb("sq1", [P, 3 * R, D])
        xn1 = sb("xn1", [P, 3 * R, D])
        st1 = sb("st1", [P, 5, 3 * R])
        x1T = sb("x1T", [D + 1, 3, NT])
        z_parts = sb("z_parts", [128, 6, NT], BF16)
        z_rest = sb("z_rest", [128, 2, NT])
        q_stack = [sb(f"q_stack{i}", [128, PAIRS, NT], BF16) for i in range(BUFS)]
        k_stack = [sb(f"k_stack{i}", [128, SIDES, PAIRS, NT], BF16) for i in range(BUFS)]
        v_aug = [sb(f"v_aug{i}", [P, SIDES * R, HEADS, 32]) for i in range(BUFS)]

        neg_max = sb("neg_max", [P, SIDES, R, HEADS])
        sh_parts = sb("sh_parts", [P, SIDES, R, 2, 3, PAIRS], BF16)
        sh_rest = sb("sh_rest", [P, SIDES, R, HEADS])
        sh_rows = sb("sh_rows", [2 * 3 * PAIRS, SIDES, NT], BF16)
        probs = sb("probs", [P, HEADS, R, NT])
        o_sb = sb("o_sb", [128, SIDES, NT])

        recip1 = sb("recip1", [P, SIDES * R, 4, 2])
        on_side = sb("on_side", [P, SIDES * R, 2, 4, DH])
        on_sum = sb("on_sum", [P, R, D])
        onT = sb("onT", [D + 1, NT])
        h1 = sb("h1", [P, R, D])
        h1b = [sb(f"h1b{i}", [P, R, D]) for i in range(BUFS)]
        xc2 = sb("xc2", [P, R, D])
        sq2 = sb("sq2", [P, R, D])
        xn2 = sb("xn2", [P, R, D])
        st2 = sb("st2", [P, 5, R])

        x2T = sb("x2T", [D + 1, NT])
        qk2 = sb("qk2", [D + 1, NT])
        v2_sb = sb("v2_sb", [P, R, D])
        nonzero = sb("nonzero", [P, R, 2])
        row_mask = sb("row_mask", [P, R])
        neg_max2 = sb("neg_max2", [P, R])
        bias2 = sb("bias2", [P, R])
        sums2 = sb("sums2", [P, R])
        recip2 = sb("recip2", [P, R])
        row_scale = sb("row_scale", [P, R])
        p2 = sb("p2", [P, R, NT])
        p2T = sb("p2T", [P, R, NT])
        o2T = sb("o2T", [2 * D, NT])
        h2 = [sb(f"h2_{i}", [P, R, D]) for i in range(BUFS)]
        xc3 = sb("xc3", [P, R, D])
        sq3 = sb("sq3", [P, R, D])
        xn3 = sb("xn3", [P, R, D])
        st3 = sb("st3", [P, 5, R])

        x3_rows = sb("x3_rows", [128, NT])
        one_hotT = sb("one_hotT", [3 * EXPERTS, NT], BF16)
        top = sb("top", [P, R])
        top_rank = sb("top_rank", [P, R, EXPERTS])
        best_rank = sb("best_rank", [P, R])
        one_hot = sb("one_hot", [P, R, 4, EXPERTS], BF16)
        hidden = sb("hidden", [128, CHUNKS, NT])
        outT = sb("outT", [2 * D, NT])
        y_sb = sb("y_sb", [P, R, D])

        consts_loaded = sem("consts_loaded")
        rows_set = sem("rows_set")
        zeros_set = sem("zeros_set")
        id16_ready = sem("id16_ready")
        b2_step = sem("b2_step")
        a2_ready, a2_taken = sem("a2_ready"), sem("a2_taken")
        x_loaded = sem("x_loaded")
        parts_stored = sem("parts_stored")
        stacks_loaded = sem("stacks_loaded")
        shift_stored = sems("shift_stored", SIDES)
        shift_loaded = sems("shift_loaded", SIDES)
        y_stored = sem("y_stored")

        def norm_sems(i):
            names = ("summed", "mean", "centered", "squared", "sumsq", "var", "rstd", "normed")
            return {n: sem(f"ln{i}_{n}") for n in names}

        ln1, ln2, ln3 = norm_sems(1), norm_sems(2), norm_sems(3)
        xT_kv_ready, xT_kv_taken = sem("xT_kv_ready"), sem("xT_kv_taken")
        xT_q_ready, xT_q_taken = sem("xT_q_ready"), sem("xT_q_taken")
        z_ready, z_high, z_rest_ready, z_mid, z_low = [sem(f"z_{n}") for n in ("ready", "high", "rest", "mid", "low")]
        v_ready, v_taken = sem("v_ready"), sem("v_taken")
        max_scores, max_done = sems("max_scores", HEADS), sems("max_done", HEADS)
        exp_scores, exp_done = sems("exp_scores", HEADS), sems("exp_done", HEADS)
        sh_high, sh_rest1, sh_mid, sh_low = [sems(f"sh_{n}", SIDES) for n in ("high", "rest", "mid", "low")]
        shT_ready, shT_taken = sems("shT_ready", SIDES), sems("shT_taken", SIDES)
        pv_done = sems("pv_done", 4)
        o_taken = sem("o_taken")
        oT_ready, o_recip, o_normed = sem("oT_ready"), sem("o_recip"), sem("o_normed")
        o_summed = sem("o_summed")
        onT_ready, onT_taken = sem("onT_ready"), sem("onT_taken")
        h1_ready, h1_taken, h1b_ready = sem("h1_ready"), sem("h1_taken"), sem("h1b_ready")
        x2T_ready, x2T_taken = sem("x2T_ready"), sem("x2T_taken")
        qk2_ready, qk2_taken = sem("qk2_ready"), sem("qk2_taken")
        v2_ready, v2_taken, nonzero_ready, mask_ready = [sem(n) for n in ("v2_ready", "v2_taken", "nonzero_ready", "mask_ready")]
        scores2_ready, max2_ready, bias2_ready, exp2_done = [sem(n) for n in ("scores2_ready", "max2_ready", "bias2_ready", "exp2_done")]
        p2T_ready, p2T_taken = sem("p2T_ready"), sem("p2T_taken")
        o2_ready, o2_taken = sem("o2_ready"), sem("o2_taken")
        recip2_ready, scale2_ready = sem("recip2_ready"), sem("scale2_ready")
        out2_ready, h2_ready = sem("out2_ready"), sem("h2_ready")
        x3T_ready, x3T_taken = sem("x3T_ready"), sem("x3T_taken")
        logits_ready, top_ready = sem("logits_ready"), sem("top_ready")
        rank_ready, best_ready, one_hot_ready = sem("rank_ready"), sem("best_ready"), sem("one_hot_ready")
        ohT_ready, ohT_taken = sem("ohT_ready"), sem("ohT_taken")
        hid_ready, relu_done = sems("hid_ready", 2), sems("relu_done", 2)
        outT_ready, outT_taken = sem("outT_ready"), sem("outT_taken")
        out_ready, y_ready = sem("out_ready"), sem("y_ready")

        N_CONST_DMAS = 12 + BUFS * 2
        PARTS_DMAS, STACK_DMAS, SHIFT_LOADS = 3, 12, 2

        def wait(eng, semaphore, value):
            if isinstance(value, int) and value <= 0:
                return
            eng.wait_ge(semaphore, value)

        def unit_count(u, b):
            return b * SIDES + u // HEADS + 1

        def before(u, by):
            return (u - by) % UNITS, (u - by) // UNITS

        def batches(t, live):
            return [t - i for i in range(DEPTH)], lambda s: s in live

        def run(iteration, loop):
            fill = DEPTH - 1
            trips = (BATCH - fill) // BUFS
            for t in range(fill):
                iteration(t, t % BUFS, STAGES[:t + 1])
            with loop(fill, fill + trips * BUFS - (BUFS - 1), BUFS) as t:
                for k in range(BUFS):
                    iteration(t + k, k, STAGES)
            for t in range(fill + trips * BUFS, BATCH + fill):
                live = "".join(s for i, s in enumerate(STAGES) if 0 <= t - i < BATCH)
                iteration(t, t % BUFS, live)

        def weight(name):
            lo, hi = COLS[name]
            return w_sb[:, lo:hi]

        block = ctx.enter_context(nc.Block())

        @block.sync
        def _(sp):
            xs = x.rearrange("n (s p r) d -> n p s r d", s=3, r=R)
            ys = out.rearrange("n (p r) d -> n p r d", r=R)
            q_rows = q_parts.rearrange("a (i m g) c -> m (a i) g c", m=2, g=PAIRS)
            k_rows = k_parts.rearrange("s a (i m g) c -> m (a i) s g c", m=2, g=PAIRS)
            TERMS = ((0, 0, 24, 0), (24, 0, 16, 8), (40, 0, 8, 16))

            def shift_io(side, batch, k):
                wait(sp, shT_taken[side], batch + 1)
                sp.dma_start(shift_parts[side].rearrange("m a g c -> (m a g) c"),
                             sh_rows[:, side, :]).then_inc(shift_stored[side], 16)
                wait(sp, shift_stored[side], batch * 16 + 16)
                for par in range(2):
                    row = 64 * par + SHIFT + 3 * side
                    sp.dma_start(q_stack[k][row:row + 3], shift_parts[side, par]).then_inc(shift_loaded[side], 16)

            def load_x(n):
                sp.dma_start(x_in[:].rearrange("p (s r) d -> p s r d", r=R),
                             xs[n] if isinstance(n, int) else xs[bass.ds(n, 1)].squeeze(0)).then_inc(x_loaded, 16)

            load_x(0)
            for dst, src in ((w_sb[:], w65), (gb_sb[:], ln_gb), (w1_sb[:], w1aug),
                             (w2_sb[:], w2.rearrange("(c p) d -> p c d", p=128)), (b2_rep[:], b2),
                             (qk2_w_sb[:], qk2_w.rearrange("c (i j) -> c i j", i=2)), (o2_w_sb[:], o2_w),
                             (bo2_sb[:], bo2.to_broadcast([P, D])), (id32[:], ident),
                             (id_twice[0:D], ident[0:D, 0:D]), (id_twice[D:], ident[0:D, 0:D]),
                             (rank_sb[:], expert_rank.to_broadcast([P, EXPERTS]))):
                sp.dma_start(dst, src).then_inc(consts_loaded, 16)
            for i in range(BUFS):
                for par in range(2):
                    sp.dma_start(k_stack[i][64 * par + SHIFT:64 * par + KROWS], shift_rows).then_inc(consts_loaded, 16)

            def iteration(t, k, live):
                (n, a, b, c, d, e, f), on = batches(t, live)
                if on("C"):
                    shift_io(1, c, (k - 3) % BUFS)
                if on("A"):
                    ka = (k - 1) % BUFS
                    wait(sp, z_low, a + 1)
                    sp.dma_start(q_parts.rearrange("a r c -> r a c"), z_parts[0:D, 0:3, :]).then_inc(parts_stored, 16)
                    for side in range(SIDES):
                        sp.dma_start(k_parts[side].rearrange("a r c -> r a c"),
                                     z_parts[D * side:D * side + D, 3:6, :]).then_inc(parts_stored, 16)
                    wait(sp, parts_stored, a * (16 * PARTS_DMAS) + 16 * PARTS_DMAS)
                    for first, q0, rows, k0 in TERMS:
                        for par in range(2):
                            at = 64 * par + first
                            sp.dma_start(q_stack[ka][at:at + rows],
                                         q_rows[par, q0:q0 + rows]).then_inc(stacks_loaded, 16)
                            sp.dma_start(k_stack[ka][at:at + rows],
                                         k_rows[par, k0:k0 + rows]).then_inc(stacks_loaded, 16)
                if on("N") and not (isinstance(n, int) and n + 1 == BATCH):
                    wait(sp, ln1["centered"], n + 1)
                    load_x(n + 1)
                if on("B"):
                    shift_io(0, b, (k - 2) % BUFS)
                if on("F"):
                    wait(sp, y_ready, f + 1)
                    sp.dma_start(ys[f] if isinstance(f, int) else ys[bass.ds(f, 1)].squeeze(0), y_sb[:]).then_inc(y_stored, 16)

            run(iteration, sp.Fori)
            sp.wait_ge(y_stored, 16 * BATCH)

        @block.tensor
        def _(pe):
            pe.wait_ge(consts_loaded, 16 * N_CONST_DMAS)
            pe.wait_ge(rows_set, 5 + 2 * BUFS)
            pe.wait_ge(zeros_set, 2 + BUFS)
            pe.wait_ge(id16_ready, 1)

            pe.matmul(m2[0:D + 1, 0:D + 1], qk2_w_sb[:, 1, :], qk2_w_sb[:, 0, :], start=True, stop=True).then_inc(a2_ready, 1)
            pe.wait_ge(a2_taken, 1)

            def max_unit(u, b, k):
                side, head = u // HEADS, u % HEADS
                at = 64 * (head % 2)
                if u == 0:
                    pe.wait_ge(stacks_loaded, b * (16 * STACK_DMAS) + 16 * STACK_DMAS)
                prior, back = before(u, 2)
                wait(pe, max_done[prior % HEADS], unit_count(prior, b + back))
                for r in range(R):
                    last = pe.matmul(max_bank[u % 2][0:P, r * NT:(r + 1) * NT],
                                     q_stack[k][at:at + SHIFT, head // 2, r * P:(r + 1) * P],
                                     k_stack[k][at:at + SHIFT, side, head // 2, :], start=True, stop=True)
                last.then_inc(max_scores[head], 1)

            def exp_unit(u, c, k):
                side, head = u // HEADS, u % HEADS
                at = 64 * (head % 2)
                rows = SHIFT + 3 * (side + 1)
                if u % HEADS == 0:
                    pe.wait_ge(shift_loaded[side], c * (16 * SHIFT_LOADS) + 16 * SHIFT_LOADS)
                prior, back = before(u, 2)
                wait(pe, exp_done[prior % HEADS], unit_count(prior, c + back))
                for kt in range(R):
                    last = pe.matmul(exp_bank[u % 2][0:P, kt * NT:(kt + 1) * NT],
                                     k_stack[k][at:at + rows, side, head // 2, kt * P:(kt + 1) * P],
                                     q_stack[k][at:at + rows, head // 2, :], start=True, stop=True)
                last.then_inc(exp_scores[head], 1)

            def pv(g, kt, c, k):
                side, half = g // 2, g % 2
                if kt == 0:
                    wait(pe, exp_done[(4 * g + 3) % HEADS], unit_count(4 * g + 3, c))
                if kt == 0 and g == 0:
                    wait(pe, v_taken, c + 1)
                    wait(pe, o_taken, c)
                for j in range(4):
                    head = 4 * half + j
                    last = pe.matmul(o_bank[32 * j:32 * j + 32, side * NT:(side + 1) * NT],
                                     v_aug[k][:, side * R + kt, head, :], probs[:, head, kt, :],
                                     start=(half == 0 and kt == 0), stop=(half == 1 and kt == R - 1),
                                     skip_group_check=True)
                if kt == R - 1:
                    last.then_inc(pv_done[g], 1)

            def transpose_tiles(dst, src, n):
                pe.transpose(dst[0:2 * D, 0:P], src[:, 0:2, :].rearrange("p r c -> p (r c)"), id32[0:P, 0:P])
                for r in range(1, n):
                    last = pe.transpose(dst[0:D, r * P:(r + 1) * P], src[:, r, :], id32[0:P, 0:P])
                return last

            def iteration(t, k, live):
                (n, a, b, c, d, e, f), on = batches(t, live)
                kb, kc, kd = (k - 2) % BUFS, (k - 3) % BUFS, (k - 4) % BUFS
                for slot in range(UNITS):
                    if on("C"):
                        exp_unit(slot, c, kc)
                    if on("B"):
                        max_unit(slot, b, kb)
                    if slot == 0 and on("A"):
                        wait(pe, xT_kv_taken, a + 1)
                        wait(pe, xT_q_taken, a + 1)
                        wait(pe, y_ready, f)
                        wait(pe, v_taken, a)
                        for i, (w, section) in enumerate((("q1", 0), ("q1", 0), ("k1", 1), ("k1", 2))):
                            half = i % 2
                            last = pe.matmul(m0[D * half:D * half + D, (i // 2) * NT:(i // 2 + 1) * NT],
                                             weight(w), x1T[:, section, :], start=True, stop=True,
                                             skip_group_check=True)
                        last.then_inc(z_ready, 1)
                    if slot == 1:
                        if on("E"):
                            wait(pe, x2T_taken, e + 1)
                            wait(pe, h2_ready, e)
                            if on("A"):
                                wait(pe, xT_q_taken, a + 1)
                            pe.matmul(m2[0:D + 1, 0:NT], a2_sb[:], x2T[:], start=True, stop=True).then_inc(qk2_ready, 1)
                    if slot == 2:
                        if on("C"):
                            wait(pe, sh_low[1], c + 1)
                            wait(pe, shT_taken[0], c + 1)
                            if on("A"):
                                wait(pe, xT_kv_taken, a + 1)
                            if on("E"):
                                wait(pe, x2T_taken, e + 1)
                            shift_turn(1)
                    if slot == 2 and on("D"):
                        pv(3, 0, d, kd)
                    if slot == 2 and on("F"):
                        wait(pe, ln3["normed"], f + 1)
                        wait(pe, y_ready, f)
                        if on("A"):
                            wait(pe, z_rest_ready, a + 1)
                        transpose_tiles(m0, xn3, R).then_inc(x3T_ready, 1)
                    if slot == 3:
                        if on("E"):
                            wait(pe, qk2_taken, e + 1)
                            for r in range(R):
                                last = pe.matmul(m2[0:P, r * (D + 2):(r + 1) * (D + 2)], x2T[:, r * P:(r + 1) * P],
                                                 weight("v2"), start=True, stop=True)
                            last.then_inc(v2_ready, 1)
                    if slot == 3 and on("D"):
                        pv(3, 1, d, kd)
                    if slot == 4 and on("F"):
                        wait(pe, x3T_taken, f + 1)
                        if on("A"):
                            wait(pe, z_rest_ready, a + 1)
                        for r in range(R):
                            last = pe.matmul(m0[0:P, r * EXPERTS:(r + 1) * EXPERTS], x3_rows[0:D + 1, r * P:(r + 1) * P],
                                             weight("router"), start=True, stop=True)
                        last.then_inc(logits_ready, 1)
                    if slot == 5:
                        if on("D"):
                            wait(pe, o_taken, d + 1)
                            if on("C"):
                                wait(pe, shT_taken[1], c + 1)
                            if on("E"):
                                wait(pe, x2T_taken, e + 1)
                            output_turn()
                        if on("E"):
                            wait(pe, v2_taken, e + 1)
                            wait(pe, nonzero_ready, e + 1)
                            for r in range(R):
                                last = pe.matmul(m2[0:P, r * NT:(r + 1) * NT], x2T[:, r * P:(r + 1) * P],
                                                 qk2[:], start=True, stop=True)
                            last.then_inc(scores2_ready, 1)
                    if slot in (6, 7) and on("C"):
                        pv(0, slot - 6, c, kc)
                    if slot == 6 and on("A"):
                        wait(pe, z_rest_ready, a + 1)
                        if on("F"):
                            wait(pe, rank_ready, f + 1)
                        for j in range(SIDES * R):
                            last = pe.matmul(m0[0:P, j * D:(j + 1) * D], x1T[:, 1 + j // R, (j % R) * P:(j % R + 1) * P],
                                             weight("v1"), start=True, stop=True)
                        last.then_inc(v_ready, 1)
                    if slot == 7 and on("D"):
                        wait(pe, o_summed, d + 1)
                        transpose_tiles(m1, on_sum, R).then_inc(onT_ready, 1)
                    if slot == 8:
                        if on("F"):
                            wait(pe, one_hot_ready, f + 1)
                            if on("A"):
                                wait(pe, v_taken, a + 1)
                            for r in range(R):
                                last = pe.matmul(m0[:, r * P:(r + 1) * P],
                                                 one_hot[:, r].rearrange("p i e -> p (i e)"), id16[0:P, 0:P],
                                                 start=True, stop=True)
                            last.then_inc(ohT_ready, 1)
                        if on("E"):
                            wait(pe, exp2_done, e + 1)
                            for kt in range(R):
                                for r in range(R):
                                    last = pe.transpose(m2[0:P, kt * NT + r * P:kt * NT + (r + 1) * P],
                                                        p2[:, r, kt * P:(kt + 1) * P], id32[0:P, 0:P])
                            last.then_inc(p2T_ready, 1)
                    if slot in (9, 11) and on("C"):
                        pv(1, (slot - 9) // 2, c, kc)
                    if slot == 9 and on("D"):
                        wait(pe, onT_taken, d + 1)
                        for r in range(R):
                            last = pe.matmul(m1[0:P, r * D:(r + 1) * D], onT[:, r * P:(r + 1) * P], weight("o1"),
                                             start=True, stop=True)
                        last.then_inc(h1_ready, 1)
                    if slot == 10:
                        if on("F"):
                            wait(pe, ohT_taken, f + 1)
                            expert_in(0)
                        if on("E"):
                            wait(pe, p2T_taken, e + 1)
                            for kt in range(R):
                                last = pe.matmul(m2[D * kt:D * kt + D, 0:NT], v2_sb[:, kt, :], p2T[:, kt, :],
                                                 start=True, stop=True, skip_group_check=True)
                            last.then_inc(o2_ready, 1)
                    if slot == 11:
                        if on("E"):
                            wait(pe, o2_taken, e + 1)
                            for r in range(R):
                                last = pe.matmul(m2[0:P, r * D:(r + 1) * D], o2T[:, r * P:(r + 1) * P],
                                                 o2_w_sb[:], start=True, stop=True)
                            last.then_inc(out2_ready, 1)
                        if on("B"):
                            wait(pe, sh_low[0], b + 1)
                            if on("C"):
                                wait(pe, shT_taken[1], c + 1)
                            if on("D"):
                                wait(pe, ln2["summed"], d + 1)
                            shift_turn(0)
                    if slot == 12:
                        if on("F"):
                            wait(pe, relu_done[0], f + 1)
                            expert_in(1)
                    if slot == 13 and on("N"):
                        wait(pe, ln1["normed"], n + 1)
                        wait(pe, xT_kv_taken, n)
                        if on("B"):
                            wait(pe, shT_taken[0], b + 1)
                        if on("D"):
                            wait(pe, ln2["summed"], d + 1)
                        transpose_tiles(m1, xn1[:, R:3 * R, :], 2 * R).then_inc(xT_kv_ready, 1)
                    if slot in (13, 15) and on("C"):
                        pv(2, (slot - 13) // 2, c, kc)
                    if slot == 13 and on("F"):
                        wait(pe, relu_done[1], f + 1)
                        for ch in range(CHUNKS):
                            at = D * (ch % 2)
                            last = pe.matmul(m0[at:at + D, 0:NT], w2_sb[:, ch, :], hidden[:, ch, :],
                                             start=(ch < 2), stop=(ch == CHUNKS - 1), skip_group_check=True)
                        last = pe.matmul(m0[0:D, 0:NT], b2_parts[:], one_hotT[:], start=False, stop=True,
                                         skip_group_check=True)
                        last.then_inc(outT_ready, 1)
                    if slot == 14 and on("N"):
                        wait(pe, xT_q_taken, n)
                        if on("E"):
                            wait(pe, h2_ready, e + 1)
                        transpose_tiles(m2, xn1[:, 0:R, :], R).then_inc(xT_q_ready, 1)
                    if slot == 14 and on("F"):
                        wait(pe, outT_taken, f + 1)
                        for r in range(R):
                            last = pe.matmul(m0[0:P, r * D:(r + 1) * D], outT[:, r * P:(r + 1) * P], id_twice[:],
                                             start=True, stop=True)
                        last.then_inc(out_ready, 1)
                    if slot == 15 and on("D"):
                        wait(pe, ln2["normed"], d + 1)
                        if on("B"):
                            wait(pe, shT_taken[0], b + 1)
                        if on("N"):
                            wait(pe, xT_kv_taken, n + 1)
                        transpose_tiles(m1, xn2, R).then_inc(x2T_ready, 1)

            def shift_turn(side):
                for r in range(R):
                    last = pe.matmul(m1[0:2 * 3 * PAIRS, r * P:(r + 1) * P],
                                     sh_parts[:, side, r].rearrange("p m a g -> p (m a g)"), id16[0:P, 0:P],
                                     start=True, stop=True)
                last.then_inc(shT_ready[side], 1)

            def output_turn():
                for side in range(SIDES):
                    for r in range(R):
                        at = (side * R + r) * 128
                        last = pe.transpose(m1[0:P, at:at + 128], o_sb[:, side, r * P:(r + 1) * P], id32[:])
                last.then_inc(oT_ready, 1)

            def expert_in(i):
                for ch in range(2):
                    at = (2 * i + ch) * 128
                    last = pe.matmul(m0[:, ch * NT:(ch + 1) * NT], w1_sb[:, at:at + 128], x3_rows[:], start=True, stop=True)
                last.then_inc(hid_ready[i], 1)

            run(iteration, pe.Fori)

        @block.scalar
        def _(act):
            act.wait_ge(consts_loaded, 16 * N_CONST_DMAS)
            act.wait_ge(rows_set, 5 + 2 * BUFS)
            act.wait_ge(zeros_set, 2 + BUFS)

            act.wait_ge(a2_ready, 1)
            act.copy(a2_sb[:], m2[0:D + 1, 0:D + 1]).then_inc(a2_taken, 1)

            def exp_unit(u, c):
                wait(act, exp_scores[u % HEADS], unit_count(u, c))
                if u % 4 == 0:
                    g = u // 4
                    wait(act, pv_done[(g + 2) % 4], c if g < 2 else c + 1)
                act.activation(probs[:, u % HEADS].rearrange("p k q -> p (k q)"), exp_bank[u % 2][0:P, 0:R * NT],
                               ACT.Exp, scale=SCALE).then_inc(exp_done[u % HEADS], 1)

            def shift_take(side, batch):
                wait(act, shT_ready[side], batch + 1)
                wait(act, shift_stored[side], batch * 16)
                act.copy(sh_rows[:, side, :], m1[0:2 * 3 * PAIRS, 0:NT]).then_inc(shT_taken[side], 1)

            def output_take(d):
                wait(act, pv_done[3], d + 1)
                wait(act, oT_ready, d)
                act.copy(o_sb[:].rearrange("p s q -> p (s q)"), o_bank[:, 0:SIDES * NT]).then_inc(o_taken, 1)

            def iteration(t, k, live):
                (n, a, b, c, d, e, f), on = batches(t, live)
                for slot in range(UNITS):
                    if on("C"):
                        exp_unit(slot, c)
                    if slot == 0 and on("A"):
                        wait(act, z_ready, a + 1)
                        wait(act, parts_stored, a * (16 * PARTS_DMAS))
                        act.copy(z_parts[:, 0:6:5, :], m0[:, 0:2 * NT].rearrange("p (i c) -> p i c", i=2)).then_inc(z_high, 1)
                    if slot == 1:
                        if on("E"):
                            wait(act, qk2_ready, e + 1)
                            wait(act, scores2_ready, e)
                            act.copy(qk2[:], m2[0:D + 1, 0:NT]).then_inc(qk2_taken, 1)
                    if slot == 2 and on("C"):
                        shift_take(1, c)
                    if slot == 2 and on("F"):
                        wait(act, x3T_ready, f + 1)
                        wait(act, hid_ready[1], f)
                        act.copy(x3_rows[0:D], m0[0:D, 0:NT]).then_inc(x3T_taken, 1)
                    if slot == 3 and on("D"):
                        output_take(d)
                    if slot == 6 and on("A"):
                        wait(act, v_ready, a + 1)
                        wait(act, pv_done[3], a - 2)
                        v1 = m0[0:P, 0:SIDES * R * D].rearrange("p (j h d) -> p j h d", h=HEADS, d=DH)
                        for half in range(2):
                            last = act.copy(v_aug[(k - 1) % BUFS][:, :, 4 * half:4 * half + 4, 16 * half:16 * half + DH],
                                            v1[:, :, 4 * half:4 * half + 4, :])
                        last.then_inc(v_taken, 1)
                    if slot == 6 and on("E"):
                        wait(act, bias2_ready, e + 1)
                        wait(act, p2T_ready, e)
                        wait(act, recip2_ready, e)
                        for r in range(R):
                            last = act.activation(p2[:, r, :], m2[0:P, r * NT:(r + 1) * NT], ACT.Exp,
                                                  bias=bias2[:, r:r + 1], scale=SCALE, accum_out=sums2[:, r:r + 1])
                        last.then_inc(exp2_done, 1)
                    if slot == 7 and on("D"):
                        wait(act, onT_ready, d + 1)
                        wait(act, h1_ready, d)
                        act.copy(onT[0:D], m1[0:D, 0:NT]).then_inc(onT_taken, 1)
                    if slot == 8 and on("F"):
                        wait(act, ohT_ready, f + 1)
                        wait(act, outT_ready, f)
                        act.copy(one_hotT[:], m0[0:3 * EXPERTS, 0:NT])
                        act.activation(x3_rows[96:128], m0[96:128, 0:NT], ACT.Copy, bias=-1.0).then_inc(ohT_taken, 1)
                    if slot == 8 and on("E"):
                        wait(act, p2T_ready, e + 1)
                        wait(act, o2_ready, e)
                        act.copy(p2T[:].rearrange("p k q -> p (k q)"), m2[0:P, 0:R * NT]).then_inc(p2T_taken, 1)
                    if slot == 10:
                        if on("F"):
                            expert_relu(0, f)
                        if on("E"):
                            wait(act, o2_ready, e + 1)
                            wait(act, out2_ready, e)
                            act.copy(o2T[:], m2[:, 0:NT]).then_inc(o2_taken, 1)
                    if slot == 11 and on("B"):
                        shift_take(0, b)
                    if slot == 12 and on("F"):
                        expert_relu(1, f)
                    if slot == 13 and on("N"):
                        wait(act, xT_kv_ready, n + 1)
                        wait(act, v_ready, n)
                        act.activation(x1T[0:D, 1:3].rearrange("p s c -> p (s c)"), m1[0:D, 0:2 * NT], ACT.Identity,
                                       bias=gb_sb[:, 1:2], scale=gb_sb[:, 0:1]).then_inc(xT_kv_taken, 1)
                    if slot == 13 and on("F"):
                        wait(act, outT_ready, f + 1)
                        wait(act, out_ready, f)
                        act.copy(outT[:], m0[:, 0:NT]).then_inc(outT_taken, 1)
                    if slot == 14 and on("N"):
                        wait(act, xT_q_ready, n + 1)
                        act.activation(x1T[0:D, 0], m2[0:D, 0:NT], ACT.Identity,
                                       bias=gb_sb[:, 1:2], scale=gb_sb[:, 0:1]).then_inc(xT_q_taken, 1)
                    if slot == 15 and on("D"):
                        wait(act, x2T_ready, d + 1)
                        wait(act, scores2_ready, d)
                        act.copy(x2T[0:D], m1[0:D, 0:NT]).then_inc(x2T_taken, 1)

            def expert_relu(i, f):
                wait(act, hid_ready[i], f + 1)
                wait(act, outT_ready, f)
                act.activation(hidden[:, 2 * i:2 * i + 2].rearrange("p h c -> p (h c)"), m0[:, 0:2 * NT],
                               ACT.Relu).then_inc(relu_done[i], 1)

            run(iteration, act.Fori)

        @block.vector
        def _(dve):
            dve.memset(x1T[D:D + 1], 1.0).then_inc(rows_set, 1)
            dve.memset(onT[D:D + 1], 2.0).then_inc(rows_set, 1)
            dve.memset(minus_half[:], -0.5).then_inc(zeros_set, 1)
            dve.memset(x2T[D:D + 1], 1.0).then_inc(rows_set, 1)
            dve.memset(x3_rows[64:96], 1.0).then_inc(rows_set, 1)
            dve.memset(h1[:], 0.0).then_inc(zeros_set, 1)
            for i in range(BUFS):
                dve.memset(v_aug[i][:], 0.0).then_inc(zeros_set, 1)
            dve.wait_ge(zeros_set, 2 + BUFS)
            for i in range(BUFS):
                for half in range(2):
                    at = 16 * half + DH
                    dve.memset(v_aug[i][:, :, 4 * half:4 * half + 4, at:at + 1], 1.0).then_inc(rows_set, 1)
            dve.wait_ge(consts_loaded, 16 * N_CONST_DMAS)
            dve.tensor_copy(id16[:], id32[:]).then_inc(id16_ready, 1)
            dve.tensor_copy(b2_parts[:], b2_rep[:]).then_inc(b2_step, 1)
            dve.wait_ge(b2_step, 1)
            dve.tensor_tensor(b2_rest[:], b2_rep[:], b2_parts[:], ALU.subtract).then_inc(b2_step, 1)
            dve.wait_ge(b2_step, 2)
            dve.tensor_copy(b2_mid[:], b2_rest[:]).then_inc(b2_step, 1)
            dve.wait_ge(b2_step, 3)
            dve.tensor_copy(b2_parts[EXPERTS:2 * EXPERTS], b2_mid[EXPERTS:2 * EXPERTS])
            dve.tensor_tensor(b2_parts[2 * EXPERTS:], b2_rest[2 * EXPERTS:], b2_mid[2 * EXPERTS:],
                              ALU.subtract).then_inc(rows_set, 1)

            def norm_sum(ln, src, st, b):
                wait(dve, ln["centered"], b)
                dve.reduce_sum(st[:, 0], src, axis=AX_X).then_inc(ln["summed"], 1)

            def norm_mean(ln, st, b):
                dve.wait_ge(ln["summed"], b + 1)
                dve.tensor_scalar(st[:, 1], st[:, 0], -1.0 / D, None, ALU.mult).then_inc(ln["mean"], 1)

            def norm_sumsq(ln, sq, st, b):
                dve.wait_ge(ln["squared"], b + 1)
                wait(dve, ln["normed"], b)
                dve.reduce_sum(st[:, 2], sq[:], axis=AX_X).then_inc(ln["sumsq"], 1)

            def norm_var(ln, st, b):
                dve.wait_ge(ln["sumsq"], b + 1)
                dve.tensor_scalar(st[:, 3], st[:, 2], 1.0 / D, LN_EPS, ALU.mult, ALU.add).then_inc(ln["var"], 1)

            def max_unit(u, b):
                side, head = u // HEADS, u % HEADS
                at = (head % 2) * PAIRS + head // 2
                dve.wait_ge(max_scores[head], unit_count(u, b))
                dve.tensor_reduce(neg_max[:, side, :, at], max_bank[u % 2][0:P, 0:R * NT].rearrange("p (r c) -> p r c", r=R),
                                  AX_X, ALU.max, negate=True).then_inc(max_done[head], 1)

            def shift_views(side):
                nm = neg_max[:, side].rearrange("p r (m g) -> p r m g", g=PAIRS)
                rest = sh_rest[:, side].rearrange("p r (m g) -> p r m g", g=PAIRS)
                return nm, rest, [sh_parts[:, side, :, :, i, :] for i in range(3)]

            def split_high(side, b):
                nm, rest, (high, mid, low) = shift_views(side)
                dve.wait_ge(max_done[HEADS - 1], unit_count(side * HEADS + HEADS - 1, b))
                wait(dve, shT_ready[side], b)
                dve.tensor_copy(high, nm).then_inc(sh_high[side], 1)

            def split_rest(side, b):
                nm, rest, (high, mid, low) = shift_views(side)
                dve.wait_ge(sh_high[side], b + 1)
                dve.tensor_tensor(rest, nm, high, ALU.subtract).then_inc(sh_rest1[side], 1)

            def split_mid(side, b):
                nm, rest, (high, mid, low) = shift_views(side)
                dve.wait_ge(sh_rest1[side], b + 1)
                dve.tensor_copy(mid, rest).then_inc(sh_mid[side], 1)

            def split_low(side, b):
                nm, rest, (high, mid, low) = shift_views(side)
                dve.wait_ge(sh_mid[side], b + 1)
                dve.tensor_tensor(low, rest, mid, ALU.subtract).then_inc(sh_low[side], 1)

            def output_recip(d):
                dve.wait_ge(oT_ready, d + 1)
                dve.reciprocal(recip1[:].rearrange("p n j h -> p (n j h)"),
                               m1[0:P, :].rearrange("p (n q) -> p n q", q=16)[:, :, DH]).then_inc(o_recip, 1)

            def output_scale(d):
                o = m1[0:P, :].rearrange("p (n j h q) -> p n j h q", n=SIDES * R, j=4, h=2)
                dve.wait_ge(o_recip, d + 1)
                for half in range(2):
                    last = dve.tensor_tensor(on_side[:, :, half], o[:, :, :, half, 0:DH],
                                             recip1[:, :, :, half].unsqueeze(3).to_broadcast([P, SIDES * R, 4, DH]), ALU.mult)
                last.then_inc(o_normed, 1)

            def output_sum(d):
                dve.wait_ge(o_normed, d + 1)
                wait(dve, onT_ready, d)
                s0, s1 = [on_side[:, s * R:(s + 1) * R].rearrange("p r h j q -> p (r h j q)") for s in range(SIDES)]
                dve.tensor_tensor(on_sum[:].rearrange("p r c -> p (r c)"), s0, s1, ALU.add).then_inc(o_summed, 1)

            def parts_rest(a):
                z = m0[:, 0:2 * NT].rearrange("p (i c) -> p i c", i=2)
                dve.wait_ge(z_high, a + 1)
                wait(dve, z_low, a)
                dve.tensor_tensor(z_rest[:], z, z_parts[:, 0:6:5, :], ALU.subtract).then_inc(z_rest_ready, 1)

            def parts_mid(a):
                dve.wait_ge(z_rest_ready, a + 1)
                dve.tensor_copy(z_parts[:, 1:5:3, :], z_rest[:]).then_inc(z_mid, 1)

            def max_2(e):
                dve.wait_ge(scores2_ready, e + 1)
                dve.tensor_reduce(neg_max2[:], m2[0:P, 0:R * NT].rearrange("p (r c) -> p r c", r=R), AX_X,
                                  ALU.max, negate=True).then_inc(max2_ready, 1)

            def bias_2(e):
                dve.wait_ge(max2_ready, e + 1)
                wait(dve, exp2_done, e)
                dve.tensor_scalar(bias2[:], neg_max2[:], SCALE, None, ALU.mult).then_inc(bias2_ready, 1)

            def recip_2(e):
                dve.wait_ge(exp2_done, e + 1)
                dve.reciprocal(recip2[:], sums2[:]).then_inc(recip2_ready, 1)

            def scale_2(e):
                dve.wait_ge(recip2_ready, e + 1)
                dve.wait_ge(mask_ready, e + 1)
                dve.tensor_tensor(row_scale[:], recip2[:], row_mask[:], ALU.mult).then_inc(scale2_ready, 1)

            def take_h1(d):
                dve.wait_ge(h1_ready, d + 1)
                wait(dve, ln2["centered"], d)
                wait(dve, h1b_ready, d)
                dve.tensor_copy(h1[:].rearrange("p r c -> p (r c)"), m1[0:P, 0:R * D]).then_inc(h1_taken, 1)

            def iteration(t, k, live):
                (n, a, b, c, d, e, f), on = batches(t, live)
                for slot in range(UNITS):
                    if slot == 0 and on("C"):
                        split_high(1, c)
                    if slot == 8 and on("B"):
                        split_high(0, b)
                    if on("B"):
                        max_unit(slot, b)
                    if slot == 0:
                        if on("C"):
                            split_rest(1, c)
                        if on("N"):
                            dve.wait_ge(x_loaded, n * 16 + 16)
                            norm_sum(ln1, x_in[:], st1, n)
                        if on("C"):
                            split_mid(1, c)
                        if on("N"):
                            norm_mean(ln1, st1, n)
                        if on("C"):
                            split_low(1, c)
                        if on("A"):
                            parts_rest(a)
                    if slot == 1 and on("A"):
                        parts_mid(a)
                    if slot == 3 and on("E"):
                        v2 = m2[0:P, 0:R * (D + 2)].rearrange("p (r c) -> p r c", r=R)
                        dve.wait_ge(v2_ready, e + 1)
                        dve.tensor_scalar(nonzero[:], v2[:, :, D:D + 2], 0.0, None, ALU.not_equal).then_inc(nonzero_ready, 1)
                        wait(dve, o2_ready, e)
                        dve.tensor_copy(v2_sb[:], v2[:, :, 0:D]).then_inc(v2_taken, 1)
                        dve.wait_ge(nonzero_ready, e + 1)
                        dve.tensor_tensor(row_mask[:], nonzero[:, :, 0], nonzero[:, :, 1], ALU.mult).then_inc(mask_ready, 1)
                    if slot == 4 and on("F"):
                        route_top(f)
                    if slot == 5:
                        if on("F"):
                            route_rank(f)
                        if on("D"):
                            output_recip(d)
                        if on("F"):
                            route_best(f)
                        if on("E"):
                            max_2(e)
                        if on("D"):
                            output_scale(d)
                        if on("E"):
                            bias_2(e)
                        if on("D"):
                            output_sum(d)
                    if slot == 6:
                        if on("F"):
                            route_one_hot(f)
                        if on("N"):
                            norm_sumsq(ln1, sq1, st1, n)
                    if slot == 7 and on("N"):
                        norm_var(ln1, st1, n)
                    if slot == 8:
                        if on("E"):
                            recip_2(e)
                        if on("B"):
                            split_rest(0, b)
                        if on("E"):
                            scale_2(e)
                        if on("B"):
                            split_mid(0, b)
                    if slot == 9:
                        if on("D"):
                            take_h1(d)
                            norm_sum(ln2, m1[0:P, 0:R * D].rearrange("p (r c) -> p r c", r=R), st2, d)
                        if on("B"):
                            split_low(0, b)
                        if on("D"):
                            norm_mean(ln2, st2, d)
                    if slot == 11:
                        if on("E"):
                            ke = (k - 5) % BUFS
                            dve.wait_ge(out2_ready, e + 1)
                            dve.wait_ge(scale2_ready, e + 1)
                            dve.wait_ge(h1b_ready, e + 1)
                            for r in range(R):
                                last = dve.scalar_tensor_tensor(out=h2[ke][:, r, :], in0=m2[0:P, r * D:(r + 1) * D],
                                                                scalar=row_scale[:, r:r + 1], in1=h1b[ke][:, r, :],
                                                                op0=ALU.mult, op1=ALU.add)
                            last.then_inc(h2_ready, 1)
                        if on("D"):
                            norm_sumsq(ln2, sq2, st2, d)
                        if on("E"):
                            dve.wait_ge(h2_ready, e + 1)
                            norm_sum(ln3, h2[ke][:], st3, e)
                        if on("D"):
                            norm_var(ln2, st2, d)
                        if on("E"):
                            norm_mean(ln3, st3, e)
                    if slot == 13 and on("E"):
                        norm_sumsq(ln3, sq3, st3, e)
                        norm_var(ln3, st3, e)
                    if slot == 14 and on("F"):
                        dve.wait_ge(out_ready, f + 1)
                        wait(dve, y_stored, f * 16)
                        dve.scalar_tensor_tensor(out=y_sb[:].rearrange("p r c -> p (r c)"), in0=m0[0:P, 0:R * D], scalar=0.0,
                                                 in1=h2[(k - 6) % BUFS][:].rearrange("p r c -> p (r c)"),
                                                 op0=ALU.max, op1=ALU.add).then_inc(y_ready, 1)

            def route_top(f):
                dve.wait_ge(logits_ready, f + 1)
                dve.reduce_max(top[:], m0[0:P, 0:R * EXPERTS].rearrange("p (r e) -> p r e", r=R),
                               axis=AX_X).then_inc(top_ready, 1)

            def route_rank(f):
                dve.wait_ge(top_ready, f + 1)
                for r in range(R):
                    last = dve.scalar_tensor_tensor(out=top_rank[:, r, :], in0=m0[0:P, r * EXPERTS:(r + 1) * EXPERTS],
                                                    scalar=top[:, r:r + 1], in1=rank_sb[:], op0=ALU.is_equal, op1=ALU.mult)
                last.then_inc(rank_ready, 1)

            def route_best(f):
                dve.wait_ge(rank_ready, f + 1)
                dve.reduce_max(best_rank[:], top_rank[:], axis=AX_X).then_inc(best_ready, 1)

            def route_one_hot(f):
                dve.wait_ge(best_ready, f + 1)
                wait(dve, ohT_ready, f)
                for r in range(R):
                    last = dve.tensor_scalar(one_hot[:, r], top_rank[:, r].unsqueeze(1).to_broadcast([P, 4, EXPERTS]),
                                             best_rank[:, r:r + 1], None, ALU.is_equal)
                last.then_inc(one_hot_ready, 1)

            run(iteration, dve.Fori)

        @block.gpsimd
        def _(pool):
            pool.wait_ge(consts_loaded, 16 * N_CONST_DMAS)
            pool.wait_ge(zeros_set, 2 + BUFS)

            def norm_center(ln, src, xc, sq, st, groups, b):
                pool.wait_ge(ln["mean"], b + 1)
                wait(pool, ln["normed"], b)
                pool.tensor_tensor(xc[:], src, st[:, 1].unsqueeze(2).to_broadcast([P, groups, D]),
                                   ALU.add).then_inc(ln["centered"], 1)
                pool.wait_ge(ln["centered"], b + 1)
                wait(pool, ln["sumsq"], b)
                pool.tensor_tensor(sq[:], xc[:], xc[:], ALU.mult).then_inc(ln["squared"], 1)

            def norm_scale(ln, xc, xn, st, groups, b, read):
                pool.wait_ge(ln["var"], b + 1)
                pool.tensor_tensor(st[:, 4], st[:, 3], minus_half[:].to_broadcast([P, groups]),
                                   ALU.pow).then_inc(ln["rstd"], 1)
                pool.wait_ge(ln["rstd"], b + 1)
                wait(pool, read, b)
                pool.tensor_tensor(xn[:], xc[:], st[:, 4].unsqueeze(2).to_broadcast([P, groups, D]),
                                   ALU.mult).then_inc(ln["normed"], 1)

            def iteration(t, k, live):
                (n, a, b, c, d, e, f), on = batches(t, live)
                if on("A"):
                    pool.wait_ge(z_mid, a + 1)
                    pool.tensor_tensor(z_parts[:, 2:4, :], z_rest[:], z_parts[:, 1:5:3, :], ALU.subtract).then_inc(z_low, 1)
                if on("N"):
                    norm_center(ln1, x_in[:], xc1, sq1, st1, 3 * R, n)
                    norm_scale(ln1, xc1, xn1, st1, 3 * R, n, xT_q_ready)
                if on("D"):
                    pool.wait_ge(h1_taken, d + 1)
                    wait(pool, h2_ready, d - 2)
                    pool.tensor_tensor(h1b[(k - 4) % BUFS][:], h1[:], bo2_sb[:].unsqueeze(1).to_broadcast([P, R, D]),
                                       ALU.add).then_inc(h1b_ready, 1)
                    norm_center(ln2, h1[:], xc2, sq2, st2, R, d)
                    norm_scale(ln2, xc2, xn2, st2, R, d, x2T_ready)
                if on("E"):
                    norm_center(ln3, h2[(k - 5) % BUFS][:], xc3, sq3, st3, R, e)
                    norm_scale(ln3, xc3, xn3, st3, R, e, x3T_ready)

            run(iteration, pool.Fori)


def kernel(**inputs):
    import numpy as np
    import concourse.bacc as bacc
    from concourse.bass_utils import run_bass_kernel_spmd

    a = {name: np.asarray(value) for name, value in inputs.items()}

    def with_bias(w, b):
        return np.concatenate([w.T, b[None, :]], axis=0)

    def by_stack_row(w):
        return w.reshape(D + 1, PAIRS, 2, DH).transpose(0, 3, 2, 1).reshape(D + 1, D)

    q2 = with_bias(a["L0_attn_Wq"], a["L0_attn_bq"])
    k2 = with_bias(a["L0_attn_Wk"], a["L0_attn_bk"])
    w65 = np.concatenate([
        by_stack_row(with_bias(a["L0_tok_Wq"], a["L0_tok_bq"])),
        by_stack_row(with_bias(a["L0_tok_Wk"], a["L0_tok_bk"])),
        with_bias(a["L0_tok_Wv"], a["L0_tok_bv"]),
        with_bias(a["L0_tok_Wo"], a["L0_tok_bo"]),
        with_bias(a["L0_attn_Wv"], a["L0_attn_bv"]), q2[:, 0:1], k2[:, 0:1],
        with_bias(a["L0_ffn_router_w"], a["L0_ffn_router_b"]),
    ], axis=1)
    expand = np.kron(np.eye(EXPERTS, dtype=np.float32), np.full((1, HID), 2.0 ** 126, np.float32))
    w1 = a["L0_ffn_W1"].transpose(1, 0, 2).reshape(D, EXPERTS * HID)
    w1aug = np.concatenate([w1, a["L0_ffn_b1"].reshape(1, -1), np.zeros((31, EXPERTS * HID), np.float32), expand])
    shift_rows = np.zeros((3 * SIDES, SIDES, PAIRS, NT), np.float32)
    for side in range(SIDES):
        shift_rows[3 * side:3 * side + 3, side] = 1.0
    arrays = {
        "x": a["x"], "w65": w65, "ln_gb": np.stack([a["L0_tok_ln_g"], a["L0_tok_ln_b"]], axis=1),
        "w1aug": w1aug, "w2": a["L0_ffn_W2"].reshape(EXPERTS * HID, D), "b2": np.tile(a["L0_ffn_b2"], (3, 1)),
        "qk2_w": np.concatenate([a["L0_attn_Wq"], a["L0_attn_bq"][:, None], a["L0_attn_Wk"], a["L0_attn_bk"][:, None]], axis=1),
        "o2_w": np.tile(a["L0_attn_Wo"].T, (2, 1)),
        "bo2": a["L0_attn_bo"][None, :], "ident": np.eye(128, dtype=np.float32),
        "expert_rank": np.arange(EXPERTS, 0, -1, dtype=np.float32)[None, :],
        "shift_rows": shift_rows.astype(mybir.dt.np(BF16)),
    }
    arrays = {name: np.ascontiguousarray(v) for name, v in arrays.items()}
    nc = bacc.Bacc("TRN2", target_bir_lowering=False, num_devices=1)
    args = [nc.dram_tensor(name, v.shape, mybir.dt.from_np(v.dtype), kind="ExternalInput").ap()
            for name, v in arrays.items()]
    out = nc.dram_tensor("out", (BATCH, NT, D), F32, kind="ExternalOutput").ap()
    audio_tower_kernel(nc, *args, out)
    result = run_bass_kernel_spmd(nc, [arrays], core_ids=[0])
    return result.results[0]["out"]
```
